# Optimizing a Trainium2 kernel written in Bass

```python
import numpy as np
import jax
import jax.numpy as jnp

def _softmax(x, axis=-1):
    return jax.nn.softmax(x, axis=axis)

def _gelu(x):
    return jax.nn.gelu(x, approximate=True)

def _silu(x):
    return jax.nn.silu(x)

def _sigmoid(x):
    return jax.nn.sigmoid(x)

def _layernorm(x, axis=-1, eps=1e-05):
    m = jnp.mean(x, axis=axis, keepdims=True)
    v = jnp.var(x, axis=axis, keepdims=True)
    return (x - m) / jnp.sqrt(v + eps)

def _scatter_add(tgt, idx, src, axis=0):
    return tgt.at[idx].add(src)

def _segment_sum(src, seg, n):
    return jax.ops.segment_sum(src, seg, n)
kernel_name = 'mk_seq_preln_d2_jaxref_r4_cd4da0'

def setup_inputs(seed: int=0):
    np.random.seed(seed)
    _w = jnp.asarray

    def _L0_attn_setup():
        import jax, jax.numpy as jnp
        import numpy as np
        BATCH, SEQ, D_MODEL = (2, 1024, 256)
        N_HEADS = 16
        HEAD_DIM = D_MODEL // N_HEADS
        WINDOW = 128
        EPS = 1e-05

        def layer_norm(x, g, b):
            m = x.mean(-1, keepdims=True)
            v = ((x - m) ** 2).mean(-1, keepdims=True)
            return (x - m) * jax.lax.rsqrt(v + EPS) * g + b

        def sliding_window_attn(q, k, v, window, scale):
            B, H, S, D = q.shape
            W = window
            C = S // W
            qc = q.reshape(B, H, C, W, D)
            kc = k.reshape(B, H, C, W, D)
            vc = v.reshape(B, H, C, W, D)
            kprev = jnp.pad(kc, ((0, 0), (0, 0), (1, 0), (0, 0), (0, 0)))[:, :, :C]
            vprev = jnp.pad(vc, ((0, 0), (0, 0), (1, 0), (0, 0), (0, 0)))[:, :, :C]
            kcat = jnp.concatenate([kprev, kc], axis=3)
            vcat = jnp.concatenate([vprev, vc], axis=3)
            scores = jnp.einsum('bhcqd,bhckd->bhcqk', qc, kcat) * scale
            i = jnp.arange(W)[:, None]
            j = jnp.arange(2 * W)[None, :]
            band = (j >= i + 1) & (j <= i + W)
            cidx = jnp.arange(C)[:, None, None]
            valid = band[None] & ((cidx > 0) | (j[None] >= W))
            scores = jnp.where(valid[None, None], scores, -jnp.inf)
            attn = jax.nn.softmax(scores, axis=-1)
            out = jnp.einsum('bhcqk,bhckd->bhcqd', attn, vcat)
            return out.reshape(B, H, S, D)
        key = jax.random.key(seed)
        ks = jax.random.split(key, 8)
        s = 0.02
        d = D_MODEL
        return {'x': jax.random.normal(ks[0], (BATCH, SEQ, d), dtype=jnp.float32), 'w_qkv': jax.random.normal(ks[1], (3 * d, d), dtype=jnp.float32) * s, 'w_o': jax.random.normal(ks[2], (d, d), dtype=jnp.float32) * s, 'ln1_g': jnp.ones((d,), jnp.float32), 'ln1_b': jnp.zeros((d,), jnp.float32), 'ln2_g': jnp.ones((d,), jnp.float32), 'ln2_b': jnp.zeros((d,), jnp.float32), 'mlp_w1': jax.random.normal(ks[3], (4 * d, d), dtype=jnp.float32) * s, 'mlp_b1': jnp.zeros((4 * d,), jnp.float32), 'mlp_w2': jax.random.normal(ks[4], (d, 4 * d), dtype=jnp.float32) * s, 'mlp_b2': jnp.zeros((d,), jnp.float32)}
    _L0_attn_in = _L0_attn_setup()

    def _L0_ffn_setup():
        import jax, jax.numpy as jnp
        import numpy as np
        DIM = 256

        def _reference_tuple_inner(x, W_r, W_k, W_v, mu_r, mu_k):
            B, T, C = x.shape
            x_prev = jnp.concatenate([jnp.zeros((B, 1, C), x.dtype), x[:, :-1, :]], axis=1)
            xr = mu_r * x + (1.0 - mu_r) * x_prev
            xk = mu_k * x + (1.0 - mu_k) * x_prev
            r = jax.nn.sigmoid(jnp.einsum('btc,dc->btd', xr, W_r))
            k = jnp.einsum('btc,dc->btd', xk, W_k)
            k_act = jnp.square(jax.nn.relu(k))
            out = r * jnp.einsum('btc,dc->btd', k_act, W_v)
            new_state = x[:, -1, :]
            return (out, new_state)
        key = jax.random.key(seed)
        ks = jax.random.split(key, 6)
        B, T, C = (8, 512, DIM)
        x = jax.random.normal(ks[0], (B, T, C), dtype=jnp.float32)
        s = 1.0 / np.sqrt(C)
        W_r = jax.random.uniform(ks[1], (C, C), jnp.float32, -s, s)
        W_k = jax.random.uniform(ks[2], (C, C), jnp.float32, -s, s)
        W_v = jax.random.uniform(ks[3], (C, C), jnp.float32, -s, s)
        mu_r = jax.random.uniform(ks[4], (C,), jnp.float32)
        mu_k = jax.random.uniform(ks[5], (C,), jnp.float32)
        return {'x': x, 'W_r': W_r, 'W_k': W_k, 'W_v': W_v, 'mu_r': mu_r, 'mu_k': mu_k}
    _L0_ffn_in = _L0_ffn_setup()

    def _L1_attn_setup():
        import jax, jax.numpy as jnp
        import numpy as np
        B, L, DM, ED, N, R, K = (2, 256, 256, 512, 16, 64, 4)
        key = jax.random.key(seed)
        ks = jax.random.split(key, 8)
        s = 0.02
        x = jax.random.normal(ks[0], (B, L, DM), jnp.float32)
        in_proj_w = jax.random.normal(ks[1], (2 * ED, DM), jnp.float32) * s
        conv_w = jax.random.normal(ks[2], (ED, 1, K), jnp.float32) * 0.3
        x_proj_w = jax.random.normal(ks[3], (R + 2 * N, ED), jnp.float32) * s
        dt_proj_w = jax.random.normal(ks[4], (ED, R), jnp.float32) * R ** (-0.5)
        dt_proj_b = jax.random.uniform(ks[5], (ED,), jnp.float32, minval=-4.6, maxval=-2.3)
        A_log = jnp.log(jnp.tile(jnp.arange(1, N + 1, dtype=jnp.float32), (ED, 1)))
        D = jnp.ones((ED,), jnp.float32)
        out_proj_w = jax.random.normal(ks[6], (DM, ED), jnp.float32) * s
        return dict(x=x, in_proj_w=in_proj_w, conv_w=conv_w, x_proj_w=x_proj_w, dt_proj_w=dt_proj_w, dt_proj_b=dt_proj_b, A_log=A_log, D=D, out_proj_w=out_proj_w)
    _L1_attn_in = _L1_attn_setup()

    def _L1_ffn_setup():
        import jax, jax.numpy as jnp
        import numpy as np
        D_MODEL = 256
        D_FF = 1024
        NUM_EXPERTS = 8
        B, N = (16, 256)
        key = jax.random.key(seed)
        ks = jax.random.split(key, 7)
        s_in = 1.0 / np.sqrt(D_MODEL)
        s_ff = 1.0 / np.sqrt(D_FF)
        return {'x': jax.random.normal(ks[0], (B, N, D_MODEL), dtype=jnp.float32), 'Wr': jax.random.uniform(ks[1], (D_MODEL, NUM_EXPERTS), jnp.float32, -s_in, s_in), 'br': jax.random.uniform(ks[2], (NUM_EXPERTS,), jnp.float32, -s_in, s_in), 'W1': jax.random.uniform(ks[3], (NUM_EXPERTS, D_MODEL, D_FF), jnp.float32, -s_in, s_in), 'b1': jax.random.uniform(ks[4], (NUM_EXPERTS, D_FF), jnp.float32, -s_in, s_in), 'W2': jax.random.uniform(ks[5], (NUM_EXPERTS, D_FF, D_MODEL), jnp.float32, -s_ff, s_ff), 'b2': jax.random.uniform(ks[6], (NUM_EXPERTS, D_MODEL), jnp.float32, -s_ff, s_ff)}
    _L1_ffn_in = _L1_ffn_setup()
    _d = {'L0_attn_x': _L0_attn_in['x'], 'L0_attn_w_qkv': _L0_attn_in['w_qkv'], 'L0_attn_w_o': _L0_attn_in['w_o'], 'L0_attn_ln1_g': _L0_attn_in['ln1_g'], 'L0_attn_ln1_b': _L0_attn_in['ln1_b'], 'L0_attn_ln2_g': _L0_attn_in['ln2_g'], 'L0_attn_ln2_b': _L0_attn_in['ln2_b'], 'L0_attn_mlp_w1': _L0_attn_in['mlp_w1'], 'L0_attn_mlp_b1': _L0_attn_in['mlp_b1'], 'L0_attn_mlp_w2': _L0_attn_in['mlp_w2'], 'L0_attn_mlp_b2': _L0_attn_in['mlp_b2'], 'L0_ffn_W_r': _L0_ffn_in['W_r'], 'L0_ffn_W_k': _L0_ffn_in['W_k'], 'L0_ffn_W_v': _L0_ffn_in['W_v'], 'L0_ffn_mu_r': _L0_ffn_in['mu_r'], 'L0_ffn_mu_k': _L0_ffn_in['mu_k'], 'L1_attn_in_proj_w': _L1_attn_in['in_proj_w'], 'L1_attn_conv_w': _L1_attn_in['conv_w'], 'L1_attn_x_proj_w': _L1_attn_in['x_proj_w'], 'L1_attn_dt_proj_w': _L1_attn_in['dt_proj_w'], 'L1_attn_dt_proj_b': _L1_attn_in['dt_proj_b'], 'L1_attn_A_log': _L1_attn_in['A_log'], 'L1_attn_D': _L1_attn_in['D'], 'L1_attn_out_proj_w': _L1_attn_in['out_proj_w'], 'L1_ffn_Wr': _L1_ffn_in['Wr'], 'L1_ffn_br': _L1_ffn_in['br'], 'L1_ffn_W1': _L1_ffn_in['W1'], 'L1_ffn_b1': _L1_ffn_in['b1'], 'L1_ffn_W2': _L1_ffn_in['W2'], 'L1_ffn_b2': _L1_ffn_in['b2']}
    _x0 = _d['L0_attn_x']
    _d['L0_attn_x'] = jax.random.normal(jax.random.fold_in(jax.random.key(seed), 1), (8, 1024, 256), dtype=_x0.dtype)
    del _x0
    return _d

def reference(L0_attn_x, L0_attn_w_qkv, L0_attn_w_o, L0_attn_ln1_g, L0_attn_ln1_b, L0_attn_ln2_g, L0_attn_ln2_b, L0_attn_mlp_w1, L0_attn_mlp_b1, L0_attn_mlp_w2, L0_attn_mlp_b2, L0_ffn_W_r, L0_ffn_W_k, L0_ffn_W_v, L0_ffn_mu_r, L0_ffn_mu_k, L1_attn_in_proj_w, L1_attn_conv_w, L1_attn_x_proj_w, L1_attn_dt_proj_w, L1_attn_dt_proj_b, L1_attn_A_log, L1_attn_D, L1_attn_out_proj_w, L1_ffn_Wr, L1_ffn_br, L1_ffn_W1, L1_ffn_b1, L1_ffn_W2, L1_ffn_b2):

    def _L0_attn_ref(x, w_qkv, w_o, ln1_g, ln1_b, ln2_g, ln2_b, mlp_w1, mlp_b1, mlp_w2, mlp_b2):
        import jax, jax.numpy as jnp
        import numpy as np
        BATCH, SEQ, D_MODEL = (2, 1024, 256)
        N_HEADS = 16
        HEAD_DIM = D_MODEL // N_HEADS
        WINDOW = 128
        EPS = 1e-05

        def layer_norm(x, g, b):
            m = x.mean(-1, keepdims=True)
            v = ((x - m) ** 2).mean(-1, keepdims=True)
            return (x - m) * jax.lax.rsqrt(v + EPS) * g + b

        def sliding_window_attn(q, k, v, window, scale):
            B, H, S, D = q.shape
            W = window
            C = S // W
            qc = q.reshape(B, H, C, W, D)
            kc = k.reshape(B, H, C, W, D)
            vc = v.reshape(B, H, C, W, D)
            kprev = jnp.pad(kc, ((0, 0), (0, 0), (1, 0), (0, 0), (0, 0)))[:, :, :C]
            vprev = jnp.pad(vc, ((0, 0), (0, 0), (1, 0), (0, 0), (0, 0)))[:, :, :C]
            kcat = jnp.concatenate([kprev, kc], axis=3)
            vcat = jnp.concatenate([vprev, vc], axis=3)
            scores = jnp.einsum('bhcqd,bhckd->bhcqk', qc, kcat) * scale
            i = jnp.arange(W)[:, None]
            j = jnp.arange(2 * W)[None, :]
            band = (j >= i + 1) & (j <= i + W)
            cidx = jnp.arange(C)[:, None, None]
            valid = band[None] & ((cidx > 0) | (j[None] >= W))
            scores = jnp.where(valid[None, None], scores, -jnp.inf)
            attn = jax.nn.softmax(scores, axis=-1)
            out = jnp.einsum('bhcqk,bhckd->bhcqd', attn, vcat)
            return out.reshape(B, H, S, D)
        B, S, D = x.shape
        H, hd = (N_HEADS, HEAD_DIM)
        scale = 1.0 / np.sqrt(hd).astype(np.float32)
        h = layer_norm(x, ln1_g, ln1_b)
        qkv = (h @ w_qkv.T).reshape(B, S, 3, H, hd)
        q = jnp.transpose(qkv[:, :, 0], (0, 2, 1, 3))
        k = jnp.transpose(qkv[:, :, 1], (0, 2, 1, 3))
        v = jnp.transpose(qkv[:, :, 2], (0, 2, 1, 3))
        attn = sliding_window_attn(q, k, v, WINDOW, scale)
        attn = jnp.transpose(attn, (0, 2, 1, 3)).reshape(B, S, D)
        x = x + attn @ w_o.T
        h = layer_norm(x, ln2_g, ln2_b)
        h = jax.nn.gelu(h @ mlp_w1.T + mlp_b1, approximate=False)
        return x + h @ mlp_w2.T + mlp_b2

    def _L0_ffn_ref(x, W_r, W_k, W_v, mu_r, mu_k):
        import jax, jax.numpy as jnp
        import numpy as np
        DIM = 256

        def _reference_tuple_inner(x, W_r, W_k, W_v, mu_r, mu_k):
            B, T, C = x.shape
            x_prev = jnp.concatenate([jnp.zeros((B, 1, C), x.dtype), x[:, :-1, :]], axis=1)
            xr = mu_r * x + (1.0 - mu_r) * x_prev
            xk = mu_k * x + (1.0 - mu_k) * x_prev
            r = jax.nn.sigmoid(jnp.einsum('btc,dc->btd', xr, W_r))
            k = jnp.einsum('btc,dc->btd', xk, W_k)
            k_act = jnp.square(jax.nn.relu(k))
            out = r * jnp.einsum('btc,dc->btd', k_act, W_v)
            new_state = x[:, -1, :]
            return (out, new_state)
        return _reference_tuple_inner(x, W_r, W_k, W_v, mu_r, mu_k)[0]

    def _L1_attn_ref(x, in_proj_w, conv_w, x_proj_w, dt_proj_w, dt_proj_b, A_log, D, out_proj_w):
        import jax, jax.numpy as jnp
        import numpy as np
        B, L, DM, ED, N, R, K = (2, 256, 256, 512, 16, 64, 4)
        xz = jnp.einsum('bld,ed->ble', x, in_proj_w)
        xp, z = (xz[..., :ED], xz[..., ED:])
        xc = jax.lax.conv_general_dilated(xp.transpose(0, 2, 1), conv_w, window_strides=(1,), padding=[(K - 1, 0)], feature_group_count=ED, dimension_numbers=('NCH', 'OIH', 'NCH'))
        xc = jax.nn.silu(xc.transpose(0, 2, 1))
        dBC = jnp.einsum('ble,fe->blf', xc, x_proj_w)
        dt, Bm, Cm = (dBC[..., :R], dBC[..., R:R + N], dBC[..., R + N:])
        delta = jax.nn.softplus(jnp.einsum('blr,er->ble', dt, dt_proj_w) + dt_proj_b)
        A = -jnp.exp(A_log)
        dA = jnp.exp(delta[..., None] * A)
        BX = delta[..., None] * Bm[:, :, None, :] * xc[..., None]

        def comb(c1, c2):
            a1, b1 = c1
            a2, b2 = c2
            return (a1 * a2, b1 * a2 + b2)
        _, hs = jax.lax.associative_scan(comb, (dA, BX), axis=1)
        y = jnp.einsum('blen,bln->ble', hs, Cm) + D * xc
        out = jnp.einsum('ble,de->bld', y * jax.nn.silu(z), out_proj_w)
        return out

    def _L1_ffn_ref(x, Wr, br, W1, b1, W2, b2):
        import jax, jax.numpy as jnp
        import numpy as np
        D_MODEL = 256
        D_FF = 1024
        NUM_EXPERTS = 8
        B, N = (16, 256)
        scores = jnp.einsum('bh,he->be', x.mean(axis=1), Wr) + br
        top1 = jnp.argmax(scores, axis=-1)
        w1 = W1[top1]
        c1 = b1[top1]
        w2 = W2[top1]
        c2 = b2[top1]
        h = jax.nn.relu(jnp.einsum('bnh,bhf->bnf', x, w1) + c1[:, None, :])
        out = jnp.einsum('bnf,bfh->bnh', h, w2) + c2[:, None, :]
        return out
    x = L0_attn_x
    x = x + _L0_attn_ref(_layernorm(x, axis=-1), L0_attn_w_qkv, L0_attn_w_o, L0_attn_ln1_g, L0_attn_ln1_b, L0_attn_ln2_g, L0_attn_ln2_b, L0_attn_mlp_w1, L0_attn_mlp_b1, L0_attn_mlp_w2, L0_attn_mlp_b2)
    x = x + _L0_ffn_ref(_layernorm(x, axis=-1), L0_ffn_W_r, L0_ffn_W_k, L0_ffn_W_v, L0_ffn_mu_r, L0_ffn_mu_k)
    x = x + _L1_attn_ref(_layernorm(x, axis=-1), L1_attn_in_proj_w, L1_attn_conv_w, L1_attn_x_proj_w, L1_attn_dt_proj_w, L1_attn_dt_proj_b, L1_attn_A_log, L1_attn_D, L1_attn_out_proj_w)
    x = x + _L1_ffn_ref(_layernorm(x, axis=-1), L1_ffn_Wr, L1_ffn_br, L1_ffn_W1, L1_ffn_b1, L1_ffn_W2, L1_ffn_b2)
    return x

_drawn_inputs = setup_inputs


def setup_inputs(seed=0):
    import zlib

    import numpy as np

    out = dict(_drawn_inputs(seed))
    spreads = {'L0_attn_ln1_g': (1.0, 0.2),
     'L0_attn_ln1_b': (0.0, 0.1),
     'L0_attn_ln2_g': (1.0, 0.2),
     'L0_attn_ln2_b': (0.0, 0.1),
     'L0_attn_mlp_b1': (0.0, 0.1),
     'L0_attn_mlp_b2': (0.0, 0.1),
     'L1_attn_D': (1.0, 0.2)}
    factors = {}
    for name, (base, spread) in spreads.items():
        noise = np.random.default_rng([zlib.crc32(name.encode()), seed]).standard_normal(out[name].shape)
        drawn = base * np.exp(spread * noise) if base else spread * noise
        out[name] = jnp.asarray(drawn.astype(out[name].dtype))
    for name, factor in factors.items():
        out[name] = (out[name] * factor).astype(out[name].dtype)
    return out
```

```python
from contextlib import ExitStack

import concourse.bass as bass
from concourse import mybir

ALU = mybir.AluOpType
ACT = mybir.ActivationFunctionType
AX = mybir.AxisListType
F32 = mybir.dt.float32
BF16 = mybir.dt.bfloat16
U32 = mybir.dt.uint32

P = 128


class Flag:

    def __init__(self, nc, ctx, name, step=1):
        self.sem = ctx.enter_context(nc.semaphore(name))
        self.step = step
        self.count = {"group": 0, "tail": 0}

    def value(self, place, at, groups):
        part, k = place
        whole = groups * self.count["group"] + self.count["tail"]
        before = at["sequence"] * whole
        if part == "group":
            before = before + at["group"] * self.count["group"]
            k = k + 1
        else:
            k = k + 1 + groups * self.count["group"]
        return (before + k) * self.step if self.step > 1 else before + k


class Queue:

    def __init__(self, program, passed, hold_each=False):
        self.program = program
        self.passed = passed
        self.hold_each = hold_each
        self.items = {"group": [], "tail": []}

    def wait(self, *flags):
        part = self.program.part
        for f in flags:
            self.items[part].append(("wait", f, (part, f.count[part])))

    def do(self, fn, signal=None, apart=False):
        part = self.program.part
        if apart and self.items[part] and self.items[part][-1][0] == "wait":
            self.items[part].append(("hold", None, None))
        self.items[part].append(("do", fn, signal))
        if signal is not None:
            signal.count[part] += 1

    def emit(self, eng, part, at, groups):
        waited = {}
        for kind, a, b in self.items[part]:
            if kind == "wait":
                if waited.get(id(a), -1) < b[1]:
                    eng.wait_ge(a.sem, a.value(b, at, groups))
                    waited[id(a)] = b[1]
                    if self.hold_each:
                        eng.sem_inc(self.passed, 1)
            elif kind == "hold":
                eng.sem_inc(self.passed, 1)
            else:
                ins = a(eng, at)
                if b is not None:
                    ins.then_inc(b.sem, b.step)


class Program:
    def __init__(self, passed):
        self.part = "group"
        self.pe, self.act, self.dve, self.pool = (Queue(self, passed[n]) for n in range(4))
        self.sp = Queue(self, passed[4], hold_each=True)


def build_block_stack(nc, d):
    BATCH, SEQ, D = d["x"].shape
    KD = D // P
    GT = 4
    G = GT * P
    GROUPS = SEQ // G
    HEADS, HD = 16, 16
    WINDOW = 128
    FF = d["mlp_w1T"].shape[1]
    KF = FF // P
    ED = d["out_wT"].shape[0]
    KE = ED // P
    NS = d["A_log"].shape[1]
    RANK = d["dt_wT"].shape[0]
    TAPS = d["conv_w"].shape[1]
    EXPERTS, _, MFF = d["W1"].shape
    KM = MFF // P
    EPS = 1e-5
    MASKED = -1e30
    QSCALE = float(HD) ** -0.5
    PAIRS = HEADS // 2
    assert WINDOW == P and SEQ % G == 0 and HD == 16

    with ExitStack() as ctx:
        def sb(name, shape, dt=F32):
            return ctx.enter_context(nc.sbuf_tensor(name, shape, dt))

        def flag(name, step=1):
            f = Flag(nc, ctx, name, step)
            flags.append(f)
            return f

        flags = []
        banks = [ctx.enter_context(nc.psum_tensor(f"bank{i}", [P, 512], F32)) for i in range(8)]
        filled = [flag(f"filled{i}") for i in range(8)]
        drained = [flag(f"drained{i}") for i in range(8)]

        w_qkv = sb("w_qkv", [P, KD, 3 * D])
        w_o = sb("w_o", [P, KD, D])
        w_1 = sb("w_1", [P, KD, FF])
        w_2 = sb("w_2", [P, KF, D])
        w_r = sb("w_r", [P, KD, D])
        w_k = sb("w_k", [P, KD, D])
        w_v = sb("w_v", [P, KD, D])
        w_in = sb("w_in", [P, KD, 2 * ED])
        w_x = sb("w_x", [P, KE, RANK + 2 * NS])
        w_dt = sb("w_dt", [RANK, ED])
        w_out = sb("w_out", [P, KE, D])
        w_route = sb("w_route", [P, KD, EXPERTS])
        b_route = sb("b_route", [1, EXPERTS])
        vecs = sb("vecs", [P, 64])
        conv_w = sb("conv_w", [P, KE, TAPS])
        conv_diag = sb("conv_diag", [P, KE, TAPS, P])
        a_neg = sb("a_neg", [P, KE, NS])
        b2_rows = sb("b2_rows", [P, D])
        ident = sb("ident", [P, P])
        ident_bf = sb("ident_bf", [P, P], BF16)
        band = sb("band", [P, 2, 2, P], BF16)
        band_first = sb("band_first", [P, 2, 2, P], BF16)
        ones_row = sb("ones_row", [1, P])
        power = sb("power", [P, GT])

        col = {}
        at_col = 0
        for name, n in (("ln1_g", KD), ("ln1_b", KD), ("ln2_g", KD), ("ln2_b", KD), ("mlp_b1", KF),
                        ("mu_r", KD), ("mu_k", KD), ("dt_b", KE), ("D", KE),
                        ("even", 1), ("odd", 1)):
            col[name] = vecs[:, at_col:at_col + n]
            at_col += n
        assert at_col <= 64

        x_in = sb("x_in", [P, GT, D])
        y = sb("y", [P, GT, D])
        z = sb("z", [P, GT, D])
        x1 = sb("x1", [P, GT, D])
        stats = sb("stats", [P, GT, 6])
        mean_var = sb("mean_var", [P, GT, 2])
        rstd = sb("rstd", [P, GT])
        nT = sb("nT", [P, KD, 1 + G])
        kT = sb("kT", [P, KD, WINDOW + G])
        v_pad = sb("v_pad", [P, 1 + GT, PAIRS, 2, 2, HD])
        neg_max = sb("neg_max", [P, HEADS])
        den = sb("den", [P, HEADS])
        rden = sb("rden", [P, HEADS])
        region_a = sb("region_a", [P, 2 * KE * G])
        region_b = sb("region_b", [P, 6 * G])
        region_c = sb("region_c", [P, 2 * KE * G])
        xpT = sb("xpT", [P, KE, TAPS - 1 + G])
        zs = sb("zs", [P, KE, G])
        xc = sb("xc", [P, KE, G])
        dbc = sb("dbc", [RANK + 2 * NS, G])
        delta = sb("delta", [P, KE, G])
        state = sb("state", [P, NS, KE])
        x3 = sb("x3", [P, GROUPS, GT, D])
        y4T = sb("y4T", [P, KD, SEQ])
        sums = sb("sums", [P, GROUPS, KD])
        last_n = sb("last_n", [P, KD, 2])
        mean = sb("mean", [P, KD])
        scores = sb("scores", [1, 8])
        top = sb("top", [1, 8])
        top_i = sb("top_i", [1, 8], U32)
        e_w1 = sb("e_w1", [P, KD, MFF])
        e_w2 = sb("e_w2", [P, KM, D])
        e_b1 = sb("e_b1", [P, KM])
        e_b2 = sb("e_b2", [1, D])

        hT = region_a[:, :].rearrange("p (f t) -> p f t", t=G)
        bx = region_a[:, :].rearrange("p (r e t) -> p r e t", r=2, e=KE)
        q_par = region_b[:, 0:4 * G].rearrange("p (a k t) -> p a k t", a=2, k=KD)
        mixT = region_b[:, 0:4 * G].rearrange("p (a k t) -> p a k t", a=2, k=KD)
        aT = region_b[:, 4 * G:6 * G].rearrange("p (k t) -> p k t", k=KD)
        u = region_b[:, 0:4 * G].rearrange("p (e t) -> p e t", e=KE)
        c_rows = region_b[:, 4 * G:6 * G].rearrange("p (r t) -> p r t", r=2)
        prob = region_c[:, 0:1024].rearrange("p (r a k) -> p r a k", r=2, a=2)
        probT = region_c[:, 1024:2048].rearrange("p (r a k) -> p r a k", r=2, a=2)
        dgs = region_c[:, 2048:2560].rearrange("p (r a k) -> p r a k", r=2, a=2)
        hc = region_c[:, :].rearrange("p (r e t) -> p r e t", r=2, e=KE)
        out_t = region_c[:, 0:GROUPS * GT * D].rearrange("p (g t c) -> p g t c", g=GROUPS, t=GT)

        s_w = ctx.enter_context(nc.semaphore("weights_landed"))
        s_pool = ctx.enter_context(nc.semaphore("gpsimd_constants"))
        s_diag = ctx.enter_context(nc.semaphore("conv_diag_built"))
        s_act = ctx.enter_context(nc.semaphore("a_neg_built"))
        s_chain = ctx.enter_context(nc.semaphore("constants_step"))
        s_dve = ctx.enter_context(nc.semaphore("vector_constants"))

        x_landed = flag("x_landed", 16)
        x_free = flag("x_free")
        f = {n: flag(n) for n in (
            "ln_stats", "ln_rstd", "ln_out", "nT_ready", "nT_read", "z_read", "y_read",
            "q_ready", "kv_ready", "qkv_used", "neg_max_ready", "prob_ready", "rden_ready",
            "diag_ready", "probT_ready", "probT_used", "prob_used", "aT_ready", "aT_used", "carry_ready",
            "y1_ready", "base_ready", "hT_ready", "hT_used", "x1_ready",
            "diff_ready", "mix_ready", "mix_used", "k_relu", "k_sq", "sig_ready", "gated",
            "x2_ready", "xp_ready", "xp_used", "zs_ready", "xc_ready", "dbc_ready", "dbc_used",
            "sp_in", "sp_exp", "sp_ln", "delta_ready", "u_ready", "c_ready", "da_ready", "bx_ready",
            "h_ready", "hc_ready", "hc_used", "state_ready", "yd_ready", "yg_ready", "yg_used",
            "x3_ready", "y4_ready", "band_ready", "zeroed",
            "mean_sum", "mean_ready", "scores_ready", "max_ready", "pick_ready",
            "w_used", "o_ready")}
        w_picked = flag("w_picked", 16)
        out_stored = flag("out_stored", 16)

        pg = Program([ctx.enter_context(nc.semaphore(f"held{n}")) for n in range(5)])
        pe, act, dve, pool, sp = pg.pe, pg.act, pg.dve, pg.pool, pg.sp

        def tokens_of(at):
            return at["sequence"] * GROUPS + at["group"]

        x_view = d["x"].rearrange("b (g t p) c -> (b g) p t c", g=GROUPS, p=P)
        out_view = d["out"].rearrange("b (g t p) c -> b g p t c", g=GROUPS, p=P)


        def normalize(src, dst, ready, free):
            dve.wait(ready)
            for t in range(GT):
                dve.do(lambda e, at, t=t: e.bn_stats(stats[:, t, :], src[:, t, :]),
                       signal=f["ln_stats"] if t == GT - 1 else None)
            dve.wait(f["ln_stats"], f["ln_rstd"])
            for t in range(GT):
                dve.do(lambda e, at, t=t: e.bn_aggr(mean_var[:, t, :], stats[:, t, :]), apart=True,
                       signal=f["ln_stats"] if t == GT - 1 else None)
            pool.wait(f["ln_stats"], f["ln_out"])
            pool.do(apart=True, fn=lambda e, at: e.tensor_scalar(rstd[:, :], mean_var[:, :, 1], EPS, None, ALU.add),
                    signal=f["ln_rstd"])
            pool.wait(f["ln_rstd"])
            pool.do(lambda e, at: e.tensor_tensor(rstd[:, :], rstd[:, :], power[:, :], ALU.pow),
                    signal=f["ln_rstd"])
            dve.wait(f["ln_rstd"], *free)
            for t in range(GT):
                dve.do(lambda e, at, t=t: e.tensor_scalar(
                    dst[:, t, :], src[:, t, :], mean_var[:, t, 0:1], rstd[:, t:t + 1],
                    ALU.subtract, ALU.mult), signal=f["ln_out"] if t == GT - 1 else None)

        def transpose_to(src, evacuate):
            pe.wait(f["ln_out"])
            for c in range(KD):
                pe.wait(drained[c])
                for t in range(GT):
                    pe.do(lambda e, at, t=t, c=c: e.transpose(
                        banks[c][:, t * P:(t + 1) * P], src[:, t, c * P:(c + 1) * P], ident[:, :]),
                        signal=filled[c] if t == GT - 1 else None)
            for c in range(KD):
                act.wait(filled[c])
                evacuate(c, banks[c])

        def product_T(bank, lhsT, rhs, parts, cols=slice(0, G), rows=P):
            pe.wait(drained[bank])
            for i in range(parts):
                pe.do(lambda e, at, i=i: e.matmul(banks[bank][0:rows, cols], lhsT(i), rhs(i),
                                                  start=(i == 0), stop=(i == parts - 1)),
                      signal=filled[bank] if i == parts - 1 else None)

        def product_rows(bank, lhsT, rhs, parts, extra=None):
            pe.wait(drained[bank])
            for j in range(2):
                n = parts + (extra is not None)
                for i in range(n):
                    a, b = (lambda i=i, j=j: (lhsT(i, j), rhs(i))) if i < parts else extra, None
                    pe.do(lambda e, at, i=i, j=j, a=a, n=n: e.matmul(
                        banks[bank][:, j * D:(j + 1) * D], a()[0], a()[1],
                        start=(i == 0), stop=(i == n - 1)),
                        signal=filled[bank] if (i == n - 1 and j == 1) else None)


        sp.wait(x_free)
        sp.do(lambda e, at: e.dma_start(x_in[:, :, :], x_view[tokens_of(at)]), signal=x_landed)
        normalize(x_in, y, x_landed, [f["base_ready"]])
        dve.wait(f["ln_out"])
        normalize(y, z, f["ln_out"], [filled[0], filled[1], f["x2_ready"]])

        act.wait(f["mix_ready"])
        act.wait(filled[0], filled[1])
        transpose_to(z, lambda c, bank: act.do(lambda e, at: e.activation(
            nT[:, c, 1:1 + G], bank[:, :], ACT.Identity, bias=col["ln1_b"][:, c:c + 1],
            scale=col["ln1_g"][:, c:c + 1]), signal=[drained[c]][0]))
        pool.wait(f["qkv_used"], f["zeroed"], f["kv_ready"])
        pool.do(apart=True, fn=lambda e, at: e.tensor_copy(kT[:, :, 0:WINDOW], kT[:, :, G:G + WINDOW]))
        pool.do(apart=True, fn=lambda e, at: e.tensor_copy(v_pad[:, 0, :, :, :, :], v_pad[:, GT, :, :, :, :]),
                signal=f["carry_ready"])

        pe.wait(drained[0], drained[1])
        for m in range(2 * KD):
            bank = 2 + m
            product_T(bank, lambda i, m=m: w_qkv[:, i, m * P:(m + 1) * P],
                      lambda i: nT[:, i, 1:1 + G], KD)
            if m < KD:
                act.wait(filled[bank], f["qkv_used"], f["yg_ready"], f["mix_used"])
                act.do(lambda e, at, m=m, bank=bank: e.activation(
                    q_par[:, 0, m, :], banks[bank][:, :], ACT.Copy, scale=col["even"]))
                act.do(lambda e, at, m=m, bank=bank: e.activation(
                    q_par[:, 1, m, :], banks[bank][:, :], ACT.Copy, scale=col["odd"]),
                    signal=drained[bank])
            else:
                dve.wait(filled[bank], f["carry_ready"])
                dve.do(lambda e, at, m=m, bank=bank: e.tensor_copy(
                    kT[:, m - KD, WINDOW:WINDOW + G], banks[bank][:, :]), signal=drained[bank])
        for n in range(GT // 2):
            bank = 6 + n
            product_rows(bank, lambda i, j, n=n: nT[:, i, 1 + (2 * n + j) * P:1 + (2 * n + j + 1) * P],
                         lambda i: w_qkv[:, i, 2 * D:3 * D], KD)
            dve.wait(filled[bank], f["carry_ready"])
            for j in range(2):
                for par in range(2):
                    dve.do(lambda e, at, n=n, j=j, par=par, bank=bank: e.tensor_copy(
                        v_pad[:, 1 + 2 * n + j, :, par, par, :],
                        banks[bank][:, j * D:(j + 1) * D].rearrange(
                            "p (a b d) -> p a b d", b=2, d=HD)[:, :, par, :]),
                        signal=drained[bank] if (j == 1 and par == 1) else None)
        dve.wait(*drained)
        dve.do(lambda e, at: e.memset(neg_max[0:1, 0:1], 0.0), signal=f["kv_ready"])

        def scores_of(c, p, n):
            bank = n % 3
            k, q = divmod(p, 4)
            rows = slice(32 * q, 32 * q + 32)
            mask = band_first if c == 0 else band
            pe.wait(drained[bank])
            pe.do(lambda e, at: e.matmul(banks[bank][:, :], ident_bf[:, :],
                                         mask[:, :, :, :].rearrange("p a b k -> p (a b k)"),
                                         start=True, stop=False, skip_group_check=True))
            for par in range(2):
                pe.do(lambda e, at, par=par: e.matmul(
                    banks[bank][:, 256 * par:256 * par + 256],
                    q_par[rows, par, k, c * P:(c + 1) * P], kT[rows, k, c * P:(c + 2) * P],
                    start=False, stop=(par == 1), skip_group_check=True),
                    signal=filled[bank] if par == 1 else None)
            dve.wait(filled[bank])
            dve.do(lambda e, at: e.tensor_reduce(
                neg_max[:, 2 * p:2 * p + 2], banks[bank][:, :].rearrange("p (a k) -> p a k", a=2),
                AX.X, ALU.max, negate=True), signal=f["neg_max_ready"])
            act.wait(f["neg_max_ready"], f["prob_used"], f["o_ready"], f["hc_used"], out_stored)
            for par in range(2):
                h = 2 * p + par
                act.do(lambda e, at, par=par, h=h: e.activation(
                    prob[:, n % 2, par, :], banks[bank][:, 256 * par:256 * par + 256], ACT.Exp,
                    bias=neg_max[:, h:h + 1], accum_out=den[:, h:h + 1]),
                    signal=f["prob_ready"])
            act.wait(f["prob_ready"])
            act.do(lambda e, at: e.sem_inc(drained[bank].sem, 0) if False else e.nop(), signal=drained[bank])
            dve.wait(f["prob_ready"])
            dve.do(lambda e, at: e.reciprocal(rden[:, 2 * p:2 * p + 2], den[:, 2 * p:2 * p + 2]),
                   signal=f["rden_ready"])
            pool.wait(f["rden_ready"], f["prob_used"])
            pool.do(lambda e, at: e.tensor_tensor(
                dgs[:, n % 2, :, :],
                ident[:, :].rearrange("p (o k) -> p o k", o=1).broadcast_to([P, 2, P]),
                rden[:, 2 * p:2 * p + 2].rearrange("p (a o) -> p a o", o=1).broadcast_to([P, 2, P]),
                ALU.mult), signal=f["diag_ready"])

        def turn(c, p, n):
            bank = 3 + n % 2
            pe.wait(drained[bank], f["diag_ready"], f["prob_ready"])
            for par in range(2):
                for half in range(2):
                    pe.do(lambda e, at, par=par, half=half: e.matmul(
                        banks[bank][:, (2 * par + half) * P:(2 * par + half + 1) * P],
                        prob[:, n % 2, par, half * P:(half + 1) * P], dgs[:, n % 2, par, :],
                        start=True, stop=True), signal=None if (par, half) != (1, 1) else filled[bank])
            eng = dve if n % 3 == 0 else act
            eng.wait(filled[bank], f["probT_used"])
            if eng is dve:
                eng.do(lambda e, at: e.tensor_copy(
                    probT[:, n % 2, :, :].rearrange("p a k -> p (a k)"), banks[bank][:, :]),
                    signal=drained[bank])
            else:
                eng.do(lambda e, at: e.activation(
                    probT[:, n % 2, :, :].rearrange("p a k -> p (a k)"), banks[bank][:, :], ACT.Copy),
                    signal=drained[bank])

        def values_of(c, p, n):
            bank = 5 + c % 2
            k, q = divmod(p, 4)
            if p == 0:
                pe.wait(drained[bank])
            pe.wait(drained[3 + n % 2])
            for i, (par, half) in enumerate(((0, 0), (0, 1), (1, 0), (1, 1))):
                last = (i == 3)
                pe.do(lambda e, at, i=i, par=par, half=half, last=last: e.matmul(
                    banks[bank][32 * q:32 * q + 32, k * P:(k + 1) * P],
                    v_pad[:, c + half, p, par, :, :].rearrange("p b d -> p (b d)"),
                    probT[:, n % 2, par, half * P:(half + 1) * P],
                    start=(i == 0), stop=last),
                    signal=f["probT_used"] if last else None)
            if p == PAIRS - 1:
                pe.do(lambda e, at: e.nop(), signal=filled[bank])
                act.wait(f["probT_used"], filled[bank], f["aT_used"])
                act.do(lambda e, at: e.activation(
                    aT[:, :, c * P:(c + 1) * P],
                    banks[bank][:, 0:KD * P].rearrange("p (k t) -> p k t", k=KD), ACT.Copy),
                    signal=drained[bank])

        pe.wait(*drained)
        pe.wait(f["kv_ready"], f["band_ready"])
        work = [(c, p) for c in range(GT) for p in range(PAIRS)]
        for n in range(len(work) + 2):
            if n < len(work):
                scores_of(*work[n], n)
            if 1 <= n <= len(work):
                turn(*work[n - 1], n - 1)
            if n >= 2:
                values_of(*work[n - 2], n - 2)
        pe.do(lambda e, at: e.nop(), signal=f["qkv_used"])

        pe.wait(drained[5], drained[6])
        for n in range(GT // 2):
            bank = n
            product_rows(bank, lambda i, j, n=n: aT[:, i, (2 * n + j) * P:(2 * n + j + 1) * P],
                         lambda i: w_o[:, i, :], KD)
            dve.wait(filled[bank], f["ln_out"])
            dve.do(lambda e, at, n=n, bank=bank: e.tensor_tensor(
                y[:, 2 * n:2 * n + 2, :].rearrange("p t c -> p (t c)"),
                banks[bank][:, :], y[:, 2 * n:2 * n + 2, :].rearrange("p t c -> p (t c)"), ALU.add),
                signal=drained[bank])
        dve.wait(drained[0], drained[1])
        dve.do(lambda e, at: e.memset(neg_max[0:1, 0:1], 0.0), signal=f["y1_ready"])
        pool.wait(f["y1_ready"], f["x2_ready"], f["x3_ready"])
        pool.do(lambda e, at: e.tensor_tensor(x1[:, :, :], x_in[:, :, :], y[:, :, :], ALU.add),
                signal=x_free)
        pool.wait(x_free)
        pool.do(lambda e, at: e.tensor_tensor(
            x1[:, :, :], x1[:, :, :],
            b2_rows[:, :].rearrange("p (o c) -> p o c", o=1).broadcast_to([P, GT, D]), ALU.add),
            signal=f["base_ready"])

        normalize(y, z, f["y1_ready"], [filled[0], filled[1]])
        act.wait(filled[7])
        transpose_to(z, lambda c, bank: act.do(lambda e, at: e.activation(
            nT[:, c, 1:1 + G], bank[:, :], ACT.Identity, bias=col["ln2_b"][:, c:c + 1],
            scale=col["ln2_g"][:, c:c + 1]), signal=drained[c]))
        pe.wait(drained[0], drained[1])
        for m in range(KF):
            bank = 2 + m % 6
            product_T(bank, lambda i, m=m: w_1[:, i, m * P:(m + 1) * P],
                      lambda i: nT[:, i, 1:1 + G], KD)
            act.wait(filled[bank], f["hT_used"], f["hc_ready"])
            act.do(lambda e, at, m=m, bank=bank: e.activation(
                hT[:, m, :], banks[bank][:, :], ACT.Gelu, bias=col["mlp_b1"][:, m:m + 1]),
                signal=drained[bank])
        pe.wait(*drained)
        for n in range(GT // 2):
            bank = n
            product_rows(bank, lambda i, j, n=n: hT[:, i, (2 * n + j) * P:(2 * n + j + 1) * P],
                         lambda i: w_2[:, i, :], KF)
            dve.wait(filled[bank], f["base_ready"])
            dve.do(lambda e, at, n=n, bank=bank: e.tensor_tensor(
                x1[:, 2 * n:2 * n + 2, :].rearrange("p t c -> p (t c)"), banks[bank][:, :],
                x1[:, 2 * n:2 * n + 2, :].rearrange("p t c -> p (t c)"), ALU.add),
                signal=drained[bank])
        pe.do(lambda e, at: e.nop(), signal=f["hT_used"])

        dve.wait(drained[0], drained[1])
        normalize(x1, z, drained[1], [filled[0], filled[1]])
        act.wait(f["hT_used"], f["mix_ready"], f["zeroed"])
        transpose_to(z, lambda c, bank: act.do(lambda e, at: e.activation(
            nT[:, c, 1:1 + G], bank[:, :], ACT.Copy), signal=drained[c]))
        act.wait(drained[0], drained[1])
        act.do(lambda e, at: e.activation(last_n[:, :, 1:2], nT[:, :, G:G + 1], ACT.Copy))
        act.do(lambda e, at: e.activation(nT[:, :, 0:1], last_n[:, :, 0:1], ACT.Copy),
               signal=f["nT_ready"])
        act.wait(f["nT_ready"])
        act.do(lambda e, at: e.activation(last_n[:, :, 0:1], last_n[:, :, 1:2], ACT.Copy),
               signal=f["nT_ready"])
        diff = region_a[:, 0:KD * G].rearrange("p (k t) -> p k t", k=KD)
        pool.wait(f["nT_ready"], drained[0], drained[1], f["hT_used"])
        pool.do(lambda e, at: e.tensor_tensor(diff, nT[:, :, 1:1 + G], nT[:, :, 0:G], ALU.subtract),
                signal=f["diff_ready"])
        dve.wait(f["diff_ready"], f["qkv_used"])
        for a, mu in enumerate(("mu_r", "mu_k")):
            for k in range(KD):
                dve.do(lambda e, at, a=a, mu=mu, k=k: e.scalar_tensor_tensor(
                    out=mixT[:, a, k, :], in0=diff[:, k, :], scalar=col[mu][:, k:k + 1],
                    in1=nT[:, k, 0:G], op0=ALU.mult, op1=ALU.add), signal=f["mix_ready"])
        pe.wait(f["mix_ready"])
        for m in range(KD):
            bank = 2 + m
            product_T(bank, lambda i, m=m: w_k[:, i, m * P:(m + 1) * P],
                      lambda i: mixT[:, 1, i, :], KD)
            act.wait(filled[bank], f["aT_used"], f["k_sq"])
            act.do(lambda e, at, m=m, bank=bank: e.activation(
                aT[:, m, :], banks[bank][:, :], ACT.Relu), signal=drained[bank])
            pool.wait(drained[bank])
            pool.do(lambda e, at, m=m: e.tensor_tensor(aT[:, m, :], aT[:, m, :], aT[:, m, :], ALU.mult),
                    signal=f["k_sq"])
        for n in range(GT // 2):
            bank = 4 + n
            product_rows(bank, lambda i, j, n=n: mixT[:, 0, i, (2 * n + j) * P:(2 * n + j + 1) * P],
                         lambda i: w_r[:, i, :], KD)
            act.wait(filled[bank])
            act.do(lambda e, at, n=n, bank=bank: e.activation(
                z[:, 2 * n:2 * n + 2, :].rearrange("p t c -> p (t c)"), banks[bank][:, :], ACT.Sigmoid),
                signal=drained[bank])
        pe.do(lambda e, at: e.nop(), signal=f["mix_used"])
        pe.wait(f["k_sq"])
        for n in range(GT // 2):
            bank = 6 + n
            product_rows(bank, lambda i, j, n=n: aT[:, i, (2 * n + j) * P:(2 * n + j + 1) * P],
                         lambda i: w_v[:, i, :], KD)
            dve.wait(filled[bank], drained[4 + n])
            dve.do(lambda e, at, n=n, bank=bank: e.tensor_tensor(
                z[:, 2 * n:2 * n + 2, :].rearrange("p t c -> p (t c)"), banks[bank][:, :],
                z[:, 2 * n:2 * n + 2, :].rearrange("p t c -> p (t c)"), ALU.mult),
                signal=drained[bank])
            dve.wait(drained[bank])
            dve.do(lambda e, at, n=n: e.tensor_tensor(
                x1[:, 2 * n:2 * n + 2, :], x1[:, 2 * n:2 * n + 2, :], z[:, 2 * n:2 * n + 2, :], ALU.add),
                signal=f["x2_ready"])
        pe.do(lambda e, at: e.nop(), signal=f["aT_used"])

        normalize(x1, z, f["x2_ready"], [f["x2_ready"]])
        act.wait(f["mix_ready"])
        transpose_to(z, lambda c, bank: act.do(lambda e, at: e.activation(
            nT[:, c, 1:1 + G], bank[:, :], ACT.Copy), signal=drained[c]))
        act.wait(f["xp_used"], f["zeroed"], f["xp_ready"])
        act.do(lambda e, at: e.activation(xpT[:, :, 0:TAPS - 1], xpT[:, :, G:G + TAPS - 1], ACT.Copy),
               signal=f["xp_ready"])
        act.wait(f["xp_ready"])
        pe.wait(drained[0], drained[1])
        for m in range(KE):
            bank = 2 + m
            product_T(bank, lambda i, m=m: w_in[:, i, m * P:(m + 1) * P],
                      lambda i: nT[:, i, 1:1 + G], KD)
            act.wait(filled[bank])
            act.do(lambda e, at, m=m, bank=bank: e.activation(
                xpT[:, m, TAPS - 1:TAPS - 1 + G], banks[bank][:, :], ACT.Copy), signal=drained[bank])
        for m in range(KE):
            bank = (6, 7, 0, 1)[m]
            product_T(bank, lambda i, m=m: w_in[:, i, ED + m * P:ED + (m + 1) * P],
                      lambda i: nT[:, i, 1:1 + G], KD)
            act.wait(filled[bank], f["yg_ready"])
            act.do(lambda e, at, m=m, bank=bank: e.activation(
                zs[:, m, :], banks[bank][:, :], ACT.Silu), signal=drained[bank])
        for m in range(KE):
            bank = 2 + m
            pe.wait(f["xp_ready"])
            product_T(bank, lambda i, m=m: conv_diag[:, m, i, :], lambda i, m=m: xpT[:, m, i:i + G], TAPS)
            act.wait(filled[bank], f["yg_ready"])
            act.do(lambda e, at, m=m, bank=bank: e.activation(
                xc[:, m, :], banks[bank][:, :], ACT.Silu), signal=drained[bank])
        pe.do(lambda e, at: e.nop(), signal=f["xp_used"])
        pe.wait(*drained)
        product_T(6, lambda i: w_x[:, i, :], lambda i: xc[:, i, :], KE, rows=RANK + 2 * NS)
        act.wait(filled[6], f["dbc_used"])
        act.do(lambda e, at: e.activation(dbc[:, :], banks[6][0:RANK + 2 * NS, :], ACT.Copy),
               signal=drained[6])
        pe.wait(drained[6])
        for m in range(KE):
            bank = 2 + m
            product_T(bank, lambda i, m=m: w_dt[:, m * P:(m + 1) * P], lambda i: dbc[0:RANK, :], 1)
            dve.wait(filled[bank], f["u_ready"], f["yg_used"])
            dve.do(lambda e, at, m=m, bank=bank: e.tensor_scalar(
                delta[:, m, :], banks[bank][:, :], col["dt_b"][:, m:m + 1], 40.0, ALU.add, ALU.min),
                signal=f["sp_in"])
            act.wait(f["sp_in"])
            act.do(lambda e, at, m=m: e.activation(delta[:, m, :], delta[:, m, :], ACT.Exp),
                   signal=f["sp_exp"])
        for m in range(KE):
            bank = 2 + m
            act.wait(f["sp_exp"])
            act.do(lambda e, at, m=m: e.activation(delta[:, m, :], delta[:, m, :], ACT.Ln, bias=1.0),
                   signal=f["sp_ln"])
            dve.wait(f["sp_ln"])
            dve.do(lambda e, at, m=m, bank=bank: e.scalar_tensor_tensor(
                out=delta[:, m, :], in0=banks[bank][:, :], scalar=col["dt_b"][:, m:m + 1],
                in1=delta[:, m, :], op0=ALU.add, op1=ALU.max), signal=drained[bank])
        dve.wait(*drained, f["mix_used"])
        dve.do(lambda e, at: e.tensor_tensor(u, delta[:, :, :], xc[:, :, :], ALU.mult), signal=f["u_ready"])

        def rows_of(bank, row):
            sel = ident[RANK:RANK + 2 * NS, RANK + row:RANK + row + 1].broadcast_to([2 * NS, P])
            pe.wait(drained[bank])
            pe.do(lambda e, at: e.matmul(banks[bank][:, :], sel, dbc[RANK:RANK + 2 * NS, :],
                                         start=True, stop=True), signal=filled[bank])

        rows_of(0, 0)
        act.wait(f["aT_used"], f["u_ready"])
        for n in range(NS):
            r = n % 2
            rows_of(1, NS + n)
            act.wait(filled[1], f["hc_ready"] if n >= 2 else f["yg_ready"])
            act.do(lambda e, at, r=r: e.activation(c_rows[:, r, :], banks[1][:, :], ACT.Copy),
                   signal=drained[1])
            dve.wait(filled[0], f["hc_ready"], f["state_ready"], f["u_ready"], f["hT_used"], f["mix_ready"])
            dve.do(lambda e, at, r=r: e.tensor_tensor(
                bx[:, r, :, :], u,
                banks[0][:, :].rearrange("p (o t) -> p o t", o=1).broadcast_to([P, KE, G]), ALU.mult),
                signal=drained[0])
            if n + 1 < NS:
                rows_of(0, n + 1)
            dve.wait(drained[0], f["zeroed"])
            for m in range(KE):
                bank = 2 + m % 2
                act.wait(drained[bank])
                act.do(lambda e, at, m=m, n=n, bank=bank: e.activation(
                    banks[bank][:, :], delta[:, m, :], ACT.Exp, scale=a_neg[:, m, n:n + 1]),
                    signal=filled[bank])
                dve.wait(filled[bank])
                dve.do(lambda e, at, m=m, n=n, r=r, bank=bank: e.tensor_tensor_scan(
                    bx[:, r, m, :], banks[bank][:, :], bx[:, r, m, :], state[:, n, m:m + 1],
                    ALU.mult, ALU.add), signal=drained[bank])
            act.wait(drained[2], drained[3])
            act.do(lambda e, at, n=n, r=r: e.activation(
                state[:, n, :], bx[:, r, :, G - 1], ACT.Copy), signal=f["state_ready"])
            pool.wait(drained[2], drained[3], drained[1], f["hc_used"])
            pool.do(lambda e, at, r=r: e.tensor_tensor(
                hc[:, r, :, :], bx[:, r, :, :],
                c_rows[:, r, :].rearrange("p (o t) -> p o t", o=1).broadcast_to([P, KE, G]), ALU.mult),
                signal=f["hc_ready"])
            for m in range(KE):
                if n == 0:
                    pe.wait(drained[4 + m])
                pe.wait(f["hc_ready"])
                pe.do(lambda e, at, m=m, n=n, r=r: e.matmul(
                    banks[4 + m][:, :], ident[:, :], hc[:, r, m, :], start=(n == 0), stop=(n == NS - 1)),
                    signal=filled[4 + m] if n == NS - 1 else f["hc_used"] if m == KE - 1 else None)
        pe.do(lambda e, at: e.nop(), signal=f["dbc_used"])
        for m in range(KE):
            dve.wait(filled[4 + m])
            dve.do(lambda e, at, m=m: e.scalar_tensor_tensor(
                out=xc[:, m, :], in0=xc[:, m, :], scalar=col["D"][:, m:m + 1], in1=banks[4 + m][:, :],
                op0=ALU.mult, op1=ALU.add), signal=drained[4 + m])
        for m in range(KE):
            dve.wait(drained[4 + m])
            dve.do(lambda e, at, m=m: e.tensor_tensor(delta[:, m, :], xc[:, m, :], zs[:, m, :], ALU.mult),
                   signal=f["yg_ready"])
        pe.wait(f["yg_ready"])
        for n in range(GT // 2):
            bank = n
            product_rows(bank, lambda i, j, n=n: delta[:, i, (2 * n + j) * P:(2 * n + j + 1) * P],
                         lambda i: w_out[:, i, :], KE)
            dve.wait(filled[bank])
            dve.do(lambda e, at, n=n, bank=bank: e.tensor_tensor(
                x1[:, 2 * n:2 * n + 2, :].rearrange("p t c -> p (t c)"), banks[bank][:, :],
                x1[:, 2 * n:2 * n + 2, :].rearrange("p t c -> p (t c)"), ALU.add),
                signal=drained[bank])
        pe.do(lambda e, at: e.nop(), signal=f["yg_used"])
        dve.wait(drained[0], drained[1])
        dve.do(lambda e, at: e.tensor_copy(x3[:, bass.ds(at["group"], 1), :, :],
                                           x1[:, :, :].rearrange("p (o t) c -> p o t c", o=1)),
               signal=f["x3_ready"])
        normalize(x1, z, f["x3_ready"], [f["x3_ready"]])
        act.wait(f["w_used"], f["mean_sum"])
        transpose_to(z, lambda c, bank: act.do(lambda e, at: e.activation(
            y4T[:, c, bass.ds(at["group"] * G, G)], bank[:, :], ACT.Copy,
            accum_out=sums[:, bass.ds(at["group"], 1), c]), signal=drained[c]))
        pool.wait(f["qkv_used"])
        pool.do(apart=True, fn=lambda e, at: e.tensor_copy(band_first[:, :, :, :], band[:, :, :, :]), signal=f["band_ready"])

        pg.part = "tail"
        dve.wait(drained[0], drained[1])
        dve.do(lambda e, at: e.tensor_tensor(mean[:, :], sums[:, 0, :], sums[:, 1, :], ALU.add),
               signal=f["mean_sum"])
        dve.wait(f["mean_sum"])
        dve.do(lambda e, at: e.tensor_scalar(mean[:, :], mean[:, :], 1.0 / SEQ, None, ALU.mult),
               signal=f["mean_ready"])
        pe.wait(f["mean_ready"], drained[0])
        for k in range(KD):
            pe.do(lambda e, at, k=k: e.matmul(banks[0][0:1, 0:EXPERTS], mean[:, k:k + 1], w_route[:, k, :],
                                              start=(k == 0), stop=False))
        pe.do(lambda e, at: e.matmul(banks[0][0:1, 0:EXPERTS], ones_row[:, 0:1], b_route[:, :],
                                     start=False, stop=True), signal=filled[0])
        dve.wait(filled[0], f["pick_ready"])
        dve.do(lambda e, at: e.tensor_copy(scores[:, :], banks[0][0:1, 0:EXPERTS]), signal=drained[0])
        dve.wait(drained[0])
        dve.do(lambda e, at: e.max(top[:, :], scores[:, :]), apart=True, signal=f["max_ready"])
        dve.wait(f["max_ready"])
        dve.do(lambda e, at: e.max_index(top_i[:, :], top[:, :], scores[:, :]), apart=True, signal=f["pick_ready"])
        sp.wait(f["pick_ready"], f["w_used"])

        def load_expert(e, at):
            pick = e.value_load(top_i[0:1, 0:1], min_val=0, max_val=EXPERTS - 1)
            at["pick"] = pick
            return e.dma_start(e_w1[:, :, :], d["W1"][bass.ds(pick, 1)].rearrange(
                "e (k p) f -> p (e k) f", p=P))

        sp.do(load_expert, apart=True, signal=w_picked)
        sp.do(lambda e, at: e.dma_start(e_w2[:, :, :], d["W2"][bass.ds(at["pick"], 1)].rearrange(
            "e (k p) f -> p (e k) f", p=P)), signal=w_picked)
        sp.do(lambda e, at: e.dma_start(e_b1[:, :], d["b1"][bass.ds(at["pick"], 1)].rearrange(
            "e p k -> (e p) k")), signal=w_picked)
        sp.do(lambda e, at: e.dma_start(e_b2[:, :], d["b2"][bass.ds(at["pick"], 1)]), signal=w_picked)
        pe.wait(w_picked, *drained)
        for g in range(GROUPS):
            for m in range(KM):
                bank = 2 + m % 6
                product_T(bank, lambda i, m=m: e_w1[:, i, m * P:(m + 1) * P],
                          lambda i, g=g: y4T[:, i, g * G:(g + 1) * G], KD)
                act.wait(filled[bank], f["hT_used"], w_picked)
                act.do(lambda e, at, m=m, bank=bank: e.activation(
                    hT[:, m, :], banks[bank][:, :], ACT.Relu, bias=e_b1[:, m:m + 1]),
                    signal=drained[bank])
            pe.wait(*drained)
            for n in range(GT // 2):
                bank = n
                product_rows(bank, lambda i, j, n=n: hT[:, i, (2 * n + j) * P:(2 * n + j + 1) * P],
                             lambda i: e_w2[:, i, :], KM, extra=lambda: (ones_row[:, :], e_b2[:, :]))
                dve.wait(filled[bank], f["hc_used"], f["x3_ready"])
                dve.do(lambda e, at, g=g, n=n, bank=bank: e.tensor_tensor(
                    out_t[:, g, 2 * n:2 * n + 2, :].rearrange("p t c -> p (t c)"), banks[bank][:, :],
                    x3[:, g, 2 * n:2 * n + 2, :].rearrange("p t c -> p (t c)"), ALU.add),
                    signal=drained[bank])
            pe.do(lambda e, at: e.nop(), signal=f["hT_used"])
            sp.wait(drained[0], drained[1])
            sp.do(lambda e, at, g=g: e.dma_start(out_view[at["sequence"], g], out_t[:, g, :, :]),
                  signal=out_stored)
        pe.do(lambda e, at: e.nop(), signal=f["w_used"])
        pool.wait(f["qkv_used"], f["state_ready"], f["nT_ready"], f["xp_used"], f["xp_ready"], f["kv_ready"],
                  f["carry_ready"], f["band_ready"], drained[2], drained[3])

        def zero_carried(e):
            e.memset(kT[:, :, G:G + WINDOW], 0.0)
            e.memset(v_pad[:, GT, :, :, :, :], 0.0)
            e.memset(last_n[:, :, :], 0.0)
            e.memset(xpT[:, :, G:G + TAPS - 1], 0.0)
            e.memset(band_first[:, :, 0, :], MASKED)
            return e.memset(state[:, :, :], 0.0)

        pool.do(apart=True, fn=lambda e, at: zero_carried(e), signal=f["zeroed"])

        block = ctx.enter_context(nc.Block())
        WEIGHTS = (
            (w_qkv[:, :, :], d["w_qkvT"].rearrange("(k p) n -> p k n", p=P)),
            (w_o[:, :, :], d["w_oT"].rearrange("(k p) n -> p k n", p=P)),
            (w_1[:, :, :], d["mlp_w1T"].rearrange("(k p) n -> p k n", p=P)),
            (w_2[:, :, :], d["mlp_w2T"].rearrange("(k p) n -> p k n", p=P)),
            (w_r[:, :, :], d["W_rT"].rearrange("(k p) n -> p k n", p=P)),
            (w_k[:, :, :], d["W_kT"].rearrange("(k p) n -> p k n", p=P)),
            (w_v[:, :, :], d["W_vT"].rearrange("(k p) n -> p k n", p=P)),
            (w_in[:, :, :], d["in_wT"].rearrange("(k p) n -> p k n", p=P)),
            (w_x[:, :, :], d["x_wT"].rearrange("(k p) n -> p k n", p=P)),
            (w_dt[:, :], d["dt_wT"]),
            (w_out[:, :, :], d["out_wT"].rearrange("(k p) n -> p k n", p=P)),
            (w_route[:, :, :], d["Wr"].rearrange("(k p) n -> p k n", p=P)),
            (b_route[:, :], d["br"]),
            (conv_w[:, :, :], d["conv_w"].rearrange("(k p) n -> p k n", p=P)),
            (a_neg[:, :, :], d["A_log"].rearrange("(k p) n -> p k n", p=P)),
            (b2_rows[:, :], d["mlp_b2"].broadcast_to([P, D])),
        ) + tuple((col[n], d[n]) for n in ("ln1_g", "ln1_b", "ln2_g", "ln2_b", "mlp_b1", "mu_r", "mu_k",
                                          "dt_b", "D"))

        def run(e, queue):
            with e.Fori(0, BATCH) as s:
                with e.Fori(0, GROUPS) as g:
                    queue.emit(e, "group", {"sequence": s, "group": g}, GROUPS)
                queue.emit(e, "tail", {"sequence": s}, GROUPS)

        def constants(e):
            e.wait_ge(s_w, 16 * len(WEIGHTS))
            e.wait_ge(s_pool, 1)
            e.wait_ge(s_dve, 3)
            e.wait_ge(s_diag, 1)
            e.wait_ge(s_act, 2)

        @block.sync
        def _(e):
            for fl in flags:
                e.sem_inc(fl.sem, fl.step)
            for dst, src in WEIGHTS:
                e.dma_start(dst, src).then_inc(s_w, 16)
            constants(e)
            run(e, sp)
            e.wait_ge(out_stored.sem, out_stored.step * (1 + BATCH * GROUPS))

        @block.gpsimd
        def _(e):
            e.memset(ident[:, :], 0.0).then_inc(s_chain, 1)
            e.memset(band[:, :, :, :], 0.0).then_inc(s_chain, 1)
            e.memset(v_pad[:, :, :, :, :, :], 0.0)
            e.memset(kT[:, :, :], 0.0)
            e.memset(ones_row[:, :], 1.0)
            e.memset(power[:, :], -0.5)
            e.memset(xpT[:, :, :], 0.0).then_inc(s_chain, 1)
            e.wait_ge(s_chain, 3)
            e.affine_select(out=ident[:, :], in_=ident[:, :], compare_op=ALU.not_equal, fill=1.0, base=0,
                            pattern=[[-1, P]], channel_multiplier=1).then_inc(s_chain, 1)
            e.affine_select(out=band[:, :, 0, :], in_=band[:, :, 0, :], compare_op=ALU.is_gt, fill=MASKED,
                            base=0, pattern=[[0, 2], [1, P]], channel_multiplier=-1).then_inc(s_chain, 1)
            e.affine_select(out=band[:, :, 1, :], in_=band[:, :, 1, :], compare_op=ALU.is_ge, fill=MASKED,
                            base=0, pattern=[[0, 2], [-1, P]], channel_multiplier=1).then_inc(s_chain, 1)
            e.wait_ge(s_chain, 6)
            e.tensor_copy(ident_bf[:, :], ident[:, :])
            e.tensor_copy(band_first[:, :, :, :], band[:, :, :, :]).then_inc(s_chain, 1)
            e.wait_ge(s_chain, 7)
            zero_carried(e).then_inc(s_pool, 1)
            constants(e)
            run(e, pool)

        @block.vector
        def _(e):
            e.memset(col["even"], 0.0).then_inc(s_dve, 1)
            e.memset(scores[:, :], 0.0)
            e.wait_ge(s_dve, 1)
            for q in range(4):
                ins = e.memset(col["even"][32 * q:32 * q + 16, :], QSCALE)
            ins.then_inc(s_dve, 1)
            e.wait_ge(s_dve, 2)
            e.tensor_scalar(col["odd"], col["even"], -1.0, QSCALE, ALU.mult, ALU.add).then_inc(s_dve, 1)
            e.wait_ge(s_w, 16 * len(WEIGHTS))
            e.wait_ge(s_pool, 1)
            for m in range(KE):
                for k in range(TAPS):
                    ins = e.tensor_scalar(conv_diag[:, m, k, :], ident[:, :], conv_w[:, m, k:k + 1], None,
                                          ALU.mult)
            ins.then_inc(s_diag, 1)
            constants(e)
            run(e, dve)

        @block.scalar
        def _(e):
            e.wait_ge(s_w, 16 * len(WEIGHTS))
            e.activation(a_neg[:, :, :], a_neg[:, :, :], ACT.Exp).then_inc(s_act, 1)
            e.wait_ge(s_act, 1)
            e.activation(a_neg[:, :, :], a_neg[:, :, :], ACT.Copy, scale=-1.0).then_inc(s_act, 1)
            constants(e)
            run(e, act)

        @block.tensor
        def _(e):
            constants(e)
            run(e, pe)


def kernel(**inputs):
    import numpy as np
    import concourse.bacc as bacc
    from concourse.bass_utils import run_bass_kernel_spmd

    a = {n: np.asarray(v) for n, v in inputs.items()}

    def columns(v):
        return np.ascontiguousarray(v.reshape(-1, P).T)

    def transposed(v):
        return np.ascontiguousarray(v.T)

    arrays = {
        "x": a["L0_attn_x"],
        "w_qkvT": transposed(a["L0_attn_w_qkv"]), "w_oT": transposed(a["L0_attn_w_o"]),
        "ln1_g": columns(a["L0_attn_ln1_g"]), "ln1_b": columns(a["L0_attn_ln1_b"]),
        "ln2_g": columns(a["L0_attn_ln2_g"]), "ln2_b": columns(a["L0_attn_ln2_b"]),
        "mlp_w1T": transposed(a["L0_attn_mlp_w1"]), "mlp_b1": columns(a["L0_attn_mlp_b1"]),
        "mlp_w2T": transposed(a["L0_attn_mlp_w2"]), "mlp_b2": a["L0_attn_mlp_b2"].reshape(1, -1),
        "W_rT": transposed(a["L0_ffn_W_r"]), "W_kT": transposed(a["L0_ffn_W_k"]),
        "W_vT": transposed(a["L0_ffn_W_v"]),
        "mu_r": columns(a["L0_ffn_mu_r"]), "mu_k": columns(a["L0_ffn_mu_k"]),
        "in_wT": transposed(a["L1_attn_in_proj_w"]),
        "conv_w": a["L1_attn_conv_w"].reshape(a["L1_attn_conv_w"].shape[0], -1),
        "x_wT": transposed(a["L1_attn_x_proj_w"]), "dt_wT": transposed(a["L1_attn_dt_proj_w"]),
        "dt_b": columns(a["L1_attn_dt_proj_b"]), "A_log": a["L1_attn_A_log"],
        "D": columns(a["L1_attn_D"]), "out_wT": transposed(a["L1_attn_out_proj_w"]),
        "Wr": a["L1_ffn_Wr"], "br": a["L1_ffn_br"].reshape(1, -1),
        "W1": a["L1_ffn_W1"],
        "b1": np.ascontiguousarray(a["L1_ffn_b1"].reshape(a["L1_ffn_b1"].shape[0], -1, P).transpose(0, 2, 1)),
        "W2": a["L1_ffn_W2"], "b2": a["L1_ffn_b2"],
    }
    nc = bacc.Bacc("TRN2", target_bir_lowering=False, num_devices=1)
    d = {n: nc.dram_tensor(f"in_{n}", v.shape, mybir.dt.from_np(v.dtype), kind="ExternalInput").ap()
         for n, v in arrays.items()}
    x = arrays["x"]
    d["out"] = nc.dram_tensor("out_y", x.shape, mybir.dt.from_np(x.dtype), kind="ExternalOutput").ap()
    build_block_stack(nc, d)
    r = run_bass_kernel_spmd(nc, [{f"in_{n}": v for n, v in arrays.items()}], core_ids=[0])
    return r.results[0]["out_y"]
```

```python
from contextlib import ExitStack

import concourse.bass as bass
from concourse import mybir

ALU = mybir.AluOpType
ACT = mybir.ActivationFunctionType
AX = mybir.AxisListType
F32 = mybir.dt.float32
BF16 = mybir.dt.bfloat16
U32 = mybir.dt.uint32

P = 128


CREDIT = 4


class Flag:

    def __init__(self, nc, ctx, name, step=1):
        self.sem = ctx.enter_context(nc.semaphore(name))
        self.step = step
        self.count = {"prologue": 0, "body": 0, "epilogue": 0}

    def value(self, place, at):
        part, k = place
        k += CREDIT
        if part != "prologue":
            k += self.count["prologue"]
        if part == "epilogue":
            k += self.count["body"] * at["rounds"]
        if part == "body":
            return (at["round"] * self.count["body"] + k) * self.step
        return k * self.step


def but(n, flag):
    return flag, n


class Queue:

    def __init__(self, program, passed, hold_each=False):
        self.program = program
        self.passed = passed
        self.hold_each = hold_each
        self.items = {"prologue": [], "body": [], "epilogue": []}

    def wait(self, *flags):
        part = self.program.part
        for f in flags:
            f, back = f if isinstance(f, tuple) else (f, 0)
            self.items[part].append(("wait", f, (part, f.count[part] - back)))

    def do(self, fn, signal=None, apart=False):
        part = self.program.part
        if apart and self.items[part] and self.items[part][-1][0] == "wait":
            self.items[part].append(("hold", None, None))
        self.items[part].append(("do", fn, signal))
        if signal is not None:
            signal.count[part] += 1

    def emit(self, eng, part, at):
        waited = {}
        for kind, a, b in self.items[part]:
            if kind == "wait":
                if waited.get(id(a), -99) < b[1]:
                    eng.wait_ge(a.sem, a.value(b, at))
                    waited[id(a)] = b[1]
                    if self.hold_each:
                        eng.sem_inc(self.passed, 1)
            elif kind == "hold":
                eng.sem_inc(self.passed, 1)
            else:
                ins = a(eng, at)
                if b is not None:
                    ins.then_inc(b.sem, b.step)


class Program:
    def __init__(self, passed):
        self.part = "prologue"
        self.pe, self.act, self.dve, self.pool = (Queue(self, passed[n]) for n in range(4))
        self.sp = Queue(self, passed[4], hold_each=True)


def interleave(long, short, long_cost, short_cost):
    done_long = done_short = 0.0
    short_left = short is not None
    for cost in long:
        done_long += cost
        while short_left and done_short / short_cost < done_long / long_cost:
            c = next(short, None)
            if c is None:
                short_left = False
            else:
                done_short += c
    if short_left:
        for _ in short:
            pass


def build_block_stack(nc, d):
    BATCH, SEQ, D = d["x"].shape
    KD = D // P
    GT = 4
    G = GT * P
    GROUPS = SEQ // G
    HEADS, HD = 16, 16
    WINDOW = 128
    FF = d["mlp_w1T"].shape[1]
    KF = FF // P
    ED = d["out_wT"].shape[0]
    KE = ED // P
    NS = d["A_log"].shape[1]
    RANK = d["dt_wT"].shape[0]
    TAPS = d["conv_w"].shape[1]
    EXPERTS, _, MFF = d["W1"].shape
    KM = MFF // P
    EPS = 1e-5
    MASKED = -1e30
    QSCALE = float(HD) ** -0.5
    PAIRS = HEADS // 2
    H = G // 2
    CB = 4
    RING, LAG = 4, 2
    ATT = 2.2
    FRONT_US, SCAN_US = 150.0, 96.0
    assert WINDOW == P and SEQ % G == 0 and HD == 16

    with ExitStack() as ctx:
        def sb(name, shape, dt=F32):
            return ctx.enter_context(nc.sbuf_tensor(name, shape, dt))

        def flag(name, step=1):
            f = Flag(nc, ctx, name, step)
            flags.append(f)
            return f

        flags = []
        banks = [ctx.enter_context(nc.psum_tensor(f"bank{i}", [P, 512], F32)) for i in range(8)]
        filled = [flag(f"filled{i}") for i in range(8)]
        drained = [flag(f"drained{i}") for i in range(8)]

        w_qkv = sb("w_qkv", [P, KD, 3 * D])
        w_o = sb("w_o", [P, KD, D])
        w_1 = sb("w_1", [P, KD, FF])
        w_2 = sb("w_2", [P, KF, D])
        w_r = sb("w_r", [P, KD, D])
        w_k = sb("w_k", [P, KD, D])
        w_v = sb("w_v", [P, KD, D])
        w_in = sb("w_in", [P, KD, 2 * ED])
        w_x = sb("w_x", [P, KE, RANK + 2 * NS])
        w_dt = sb("w_dt", [RANK, ED])
        w_out = sb("w_out", [P, KE, D])
        w_route = sb("w_route", [P, KD, EXPERTS])
        b_route = sb("b_route", [1, EXPERTS])
        vecs = sb("vecs", [P, 64])
        conv_w = sb("conv_w", [P, KE, TAPS])
        conv_diag = sb("conv_diag", [P, KE, TAPS, P])
        a_neg = sb("a_neg", [P, KE, NS])
        b2_rows = sb("b2_rows", [P, D])
        ident = sb("ident", [P, P])
        ident_bf = sb("ident_bf", [P, P], BF16)
        band = sb("band", [P, 2, 2, P], BF16)
        band_first = sb("band_first", [P, 2, 2, P], BF16)
        ones_row = sb("ones_row", [1, P])
        power = sb("power", [P, GT])
        spare = sb("spare", [P, 4])

        col = {}
        at_col = 0
        for name, n in (("ln1_g", KD), ("ln1_b", KD), ("ln2_g", KD), ("ln2_b", KD), ("mlp_b1", KF),
                        ("mu_r", KD), ("mu_k", KD), ("dt_b", KE), ("D", KE),
                        ("even", 1), ("odd", 1)):
            col[name] = vecs[:, at_col:at_col + n]
            at_col += n
        assert at_col <= 64

        x_in = sb("x_in", [P, GT, D])
        y = sb("y", [P, GT, D])
        z = sb("z", [P, GT, D])
        ao = z[:, :, :].rearrange("p t c -> p (t c)").rearrange("p (r a k t) -> p r a k t", r=2, a=2, k=KD)
        x1 = sb("x1", [P, GROUPS, GT, D])
        stats = sb("stats", [P, GT, 6])
        mean_var = sb("mean_var", [P, GT, 2])
        rstd = sb("rstd", [P, GT])
        nT = sb("nT", [P, KD, 1 + G])
        last_n = sb("last_n", [P, KD, 1])
        kT = sb("kT", [P, KD, WINDOW + G])
        v_pad = sb("v_pad", [P, 1 + GT, PAIRS, 2, 2, HD])
        neg_max = sb("neg_max", [P, HEADS])
        den = sb("den", [P, 2, HEADS])
        rden = sb("rden", [P, HEADS])
        rden_wide = sb("rden_wide", [P, D])
        aT = sb("aT", [P, KD, G])
        probT = sb("probT", [P, 2, 2, 2 * P])
        region_f = sb("region_f", [P, KF * G])
        q_par = region_f[:, 0:4 * G].rearrange("p (a k t) -> p a k t", a=2, k=KD)
        prob = region_f[:, 4 * G:4 * G + 2048].rearrange("p (r a k) -> p r a k", r=RING, a=2)
        hT = region_f[:, 0:KF * G].rearrange("p (f t) -> p f t", t=G)
        mixT = region_f[:, 0:4 * G].rearrange("p (a k t) -> p a k t", a=2, k=KD)
        diff = region_f[:, 4 * G:6 * G].rearrange("p (k t) -> p k t", k=KD)
        xp_tail = sb("xp_tail", [P, KE, TAPS - 1])
        zs = sb("zs", [P, KE, G])
        xc = sb("xc", [P, KE, G])
        dbc = sb("dbc", [RANK + 2 * NS, G])
        delta = sb("delta", [P, KE, G])
        u = sb("u", [P, KE, G])
        state = sb("state", [P, NS, KE])
        region_s = sb("region_s", [P, 4 * KE * H])
        bx = region_s[:, 0:2 * KE * H].rearrange("p (r e t) -> p r e t", r=2, e=KE)
        hc = region_s[:, 2 * KE * H:4 * KE * H].rearrange("p (r e t) -> p r e t", r=2, e=KE)
        xpT = region_s[:, 0:KE * (TAPS - 1 + G)].rearrange("p (e t) -> p e t", e=KE)
        c_rows = sb("c_rows", [P, 2, CB, H])
        decay = sb("decay", [P, RING, 2, H])
        x3 = sb("x3", [P, GROUPS, GT, D])
        y4T = sb("y4T", [P, KD, SEQ])
        sums = sb("sums", [P, GROUPS, KD])
        mean = sb("mean", [P, KD])
        scores = sb("scores", [1, 8])
        top = sb("top", [1, 8])
        top_i = sb("top_i", [1, 8], U32)
        e_b1 = sb("e_b1", [P, KM])
        e_b2 = sb("e_b2", [1, D])
        c_dram = nc.dram_tensor("c_rows_dram", (NS, G), F32, kind="Internal").ap()

        s_w = ctx.enter_context(nc.semaphore("weights_landed"))
        s_pool = ctx.enter_context(nc.semaphore("gpsimd_constants"))
        s_diag = ctx.enter_context(nc.semaphore("conv_diag_built"))
        s_act = ctx.enter_context(nc.semaphore("a_neg_built"))
        s_chain = ctx.enter_context(nc.semaphore("constants_step"))
        s_dve = ctx.enter_context(nc.semaphore("vector_constants"))

        x_landed = flag("x_landed", 16)
        c_stored = flag("c_stored", 16)
        c_landed = [flag(f"c_landed{i}", 16) for i in range(2)]
        w_picked = flag("w_picked", 16)
        w_back = flag("w_back", 16)
        out_stored = flag("out_stored", 16)
        f = {n: flag(n) for n in (
            "ln_stats", "ln_rstd", "ln_out", "carry_in",
            "neg_max_ready", "rden_ready", "rden_wide_ready",
            "aT_ready", "y1_ready", "base_sum", "base_ready", "x1_ready",
            "last_ready", "front_zero", "diff_ready", "mix_ready", "k_sq", "gated", "x2_ready",
            "xp_ready", "tail_ready", "xc_ready", "sp_in", "sp_exp", "sp_ln", "u_ready",
            "bx_ready", "h_used", "decay_ready", "h_ready", "hc_ready", "hc_used", "state_ready", "yd_ready", "yg_ready",
            "mean_sum", "mean_ready", "max_ready", "pick_ready", "out_ready")}

        pg = Program([ctx.enter_context(nc.semaphore(f"held{n}")) for n in range(5)])
        pe, act, dve, pool, sp = pg.pe, pg.act, pg.dve, pg.pool, pg.sp

        x_view = d["x"].rearrange("b (g t p) c -> (b g) p t c", g=GROUPS, p=P)
        out_view = d["out"].rearrange("b (g t p) c -> (b g) p t c", g=GROUPS, p=P)

        def flat(ap):
            return ap.rearrange("p t c -> p (t c)")


        def normalize(src, dst, ready, free=()):
            dve.wait(ready, f["ln_stats"], f["ln_rstd"])
            for t in range(GT):
                dve.do(lambda e, at, t=t: e.bn_stats(stats[:, t, :], src[:, t, :]),
                       signal=f["ln_stats"] if t == GT - 1 else None)
            dve.wait(f["ln_stats"])
            for t in range(GT):
                dve.do(lambda e, at, t=t: e.bn_aggr(mean_var[:, t, :], stats[:, t, :]), apart=True,
                       signal=f["ln_stats"] if t == GT - 1 else None)
            pool.wait(f["ln_stats"], f["ln_out"])
            pool.do(lambda e, at: e.tensor_scalar(rstd[:, :], mean_var[:, :, 1], EPS, None, ALU.add),
                    apart=True, signal=f["ln_rstd"])
            pool.wait(f["ln_rstd"])
            pool.do(lambda e, at: e.tensor_tensor(rstd[:, :], rstd[:, :], power[:, :], ALU.pow),
                    signal=f["ln_rstd"])
            dve.wait(f["ln_rstd"], *filled[0:4], *free)
            for t in range(GT):
                dve.do(lambda e, at, t=t: e.tensor_scalar(
                    dst[:, t, :], src[:, t, :], mean_var[:, t, 0:1], rstd[:, t:t + 1],
                    ALU.subtract, ALU.mult), signal=f["ln_out"] if t == GT - 1 else None)

        def transposed(src, pair, evacuate):
            pe.wait(f["ln_out"])
            for c in range(KD):
                bank = pair[c]
                pe.wait(drained[bank])
                for t in range(GT):
                    pe.do(lambda e, at, t=t, c=c, bank=bank: e.transpose(
                        banks[bank][:, t * P:(t + 1) * P], src[:, t, c * P:(c + 1) * P], ident[:, :]),
                        signal=filled[bank] if t == GT - 1 else None)
            for c in range(KD):
                act.wait(filled[pair[c]])
                act.do(evacuate(c, banks[pair[c]]), signal=drained[pair[c]])

        def product_T(bank, lhsT, rhs, parts, rows=P):
            pe.wait(drained[bank])
            for i in range(parts):
                pe.do(lambda e, at, i=i: e.matmul(banks[bank][0:rows, :], lhsT(i), rhs(i),
                                                  start=(i == 0), stop=(i == parts - 1)),
                      signal=filled[bank] if i == parts - 1 else None)

        def product_rows(bank, n, srcT, weight, parts, bias=None):
            pe.wait(drained[bank])
            for j in range(2):
                t = 2 * n + j
                for i in range(parts):
                    pe.do(lambda e, at, i=i, j=j, t=t: e.matmul(
                        banks[bank][:, j * D:(j + 1) * D], srcT(i, slice(t * P, (t + 1) * P)), weight(i),
                        start=(i == 0), stop=(i == parts - 1 and bias is None)),
                        signal=filled[bank] if (j == 1 and i == parts - 1 and bias is None) else None)
                if bias is not None:
                    pe.do(lambda e, at, j=j: e.matmul(
                        banks[bank][:, j * D:(j + 1) * D], ones_row[:, :], bias, start=False, stop=True),
                        signal=filled[bank] if j == 1 else None)

        def tiles(t, n):
            return flat(t[:, 2 * n:2 * n + 2, :])

        ROWS_B, Y = (4, 5), (6, 7)


        def front(s, g, prefetch):
            normalize(x_in, y, x_landed, [f["base_ready"]])
            dve.wait(f["ln_out"])
            yield 6
            normalize(y, z, f["ln_out"], [f["x2_ready"]])
            yield 6
            transposed(z, (0, 1), lambda c, bank: lambda e, at: e.activation(
                nT[:, c, 1:1 + G], bank[:, :], ACT.Identity, bias=col["ln1_b"][:, c:c + 1],
                scale=col["ln1_g"][:, c:c + 1]))
            pool.wait(*filled[0:4], drained[3])
            if g == 0:
                pool.do(lambda e, at: e.memset(kT[:, :, 0:WINDOW], 0.0), apart=True)
                pool.do(lambda e, at: e.memset(v_pad[:, 0, :, :, :, :], 0.0), signal=f["carry_in"])
            else:
                pool.do(lambda e, at: e.tensor_copy(kT[:, :, 0:WINDOW], kT[:, :, G:G + WINDOW]), apart=True)
                pool.do(lambda e, at: e.tensor_copy(v_pad[:, 0, :, :, :, :], v_pad[:, GT, :, :, :, :]),
                        signal=f["carry_in"])
            yield 4
            pe.wait(drained[0], drained[1])
            for m in range(2 * KD):
                bank = (2, 3, 0, 1)[m]
                product_T(bank, lambda i, m=m: w_qkv[:, i, m * P:(m + 1) * P],
                          lambda i: nT[:, i, 1:1 + G], KD)
                if m < KD:
                    act.wait(filled[bank])
                    for par, keep in enumerate(("even", "odd")):
                        act.do(lambda e, at, m=m, bank=bank, par=par, keep=keep: e.activation(
                            q_par[:, par, m, :], banks[bank][:, :], ACT.Copy, scale=col[keep]),
                            signal=drained[bank] if par else None)
                else:
                    dve.wait(filled[bank], f["carry_in"])
                    dve.do(lambda e, at, m=m, bank=bank: e.tensor_copy(
                        kT[:, m - KD, WINDOW:WINDOW + G], banks[bank][:, :]), signal=drained[bank])
                yield 1
            for n in range(GT // 2):
                bank = 2 + n
                product_rows(bank, n, lambda i, t: nT[:, i, 1 + t.start:1 + t.stop],
                             lambda i: w_qkv[:, i, 2 * D:3 * D], KD)
                dve.wait(filled[bank], f["carry_in"])
                for par in range(2):
                    dve.do(lambda e, at, n=n, par=par, bank=bank: e.tensor_copy(
                        v_pad[:, 1 + 2 * n:3 + 2 * n, :, par, par, :],
                        banks[bank][:, :].rearrange("p (t a b d) -> p t a b d", t=2, b=2, d=HD)[:, :, :, par, :]),
                        signal=drained[bank] if par else None)
                yield 1.5
            work = [(c, p) for c in range(GT) for p in range(PAIRS)]
            pe.wait(*drained[0:4])

            def scores_of(n):
                c, p = work[n]
                bank, r = n % 2, n % RING
                k, q = divmod(p, 4)
                rows = slice(32 * q, 32 * q + 32)
                mask = band_first if (g == 0 and c == 0) else band
                pe.wait(drained[bank])
                pe.do(lambda e, at: e.matmul(banks[bank][:, :], ident_bf[:, :],
                                             mask[:, :, :, :].rearrange("p a b k -> p (a b k)"),
                                             start=True, stop=False, skip_group_check=True))
                for par in range(2):
                    pe.do(lambda e, at, par=par: e.matmul(
                        banks[bank][:, 256 * par:256 * par + 256],
                        q_par[rows, par, k, c * P:(c + 1) * P], kT[rows, k, c * P:(c + 2) * P],
                        start=False, stop=(par == 1), skip_group_check=True),
                        signal=filled[bank] if par == 1 else None)
                dve.wait(filled[bank])
                dve.do(lambda e, at: e.tensor_reduce(
                    neg_max[:, 2 * p:2 * p + 2], banks[bank][:, :].rearrange("p (a k) -> p a k", a=2),
                    AX.X, ALU.max, negate=True), signal=f["neg_max_ready"])
                act.wait(f["neg_max_ready"], but(RING - LAG, filled[2]))
                for par in range(2):
                    h = 2 * p + par
                    act.do(lambda e, at, par=par, h=h: e.activation(
                        prob[:, r, par, :], banks[bank][:, 256 * par:256 * par + 256], ACT.Exp,
                        bias=neg_max[:, h:h + 1], accum_out=den[:, c % 2, h:h + 1]),
                        signal=drained[bank] if par else None)

            def turn(n):
                bank, r = 2, n % RING
                pe.wait(drained[bank], drained[n % 2])
                for par in range(2):
                    for half in range(2):
                        pe.do(lambda e, at, par=par, half=half: e.transpose(
                            banks[bank][:, (2 * par + half) * P:(2 * par + half + 1) * P],
                            prob[:, r, par, half * P:(half + 1) * P], ident[:, :]),
                            signal=filled[bank] if par and half else None)
                act.wait(filled[bank])
                act.do(lambda e, at: e.activation(
                    flat(probT[:, n % 2, :, :]), banks[bank][:, :], ACT.Copy), signal=drained[bank])

            def values_of(n):
                c, p = work[n]
                bank = 3
                k, q = divmod(p, 4)
                if p == 0:
                    pe.wait(drained[bank])
                pe.wait(drained[2])
                for i, (par, half) in enumerate(((0, 0), (0, 1), (1, 0), (1, 1))):
                    pe.do(lambda e, at, i=i, par=par, half=half: e.matmul(
                        banks[bank][32 * q:32 * q + 32, k * P:(k + 1) * P],
                        v_pad[:, c + half, p, par, :, :].rearrange("p b d -> p (b d)"),
                        probT[:, n % 2, par, half * P:(half + 1) * P],
                        start=(i == 0), stop=(i == 3)))
                if p == PAIRS - 1:
                    pe.wait(f["rden_wide_ready"])
                    for k in range(KD):
                        pe.do(lambda e, at, k=k: e.matmul(
                            banks[bank][:, (KD + k) * P:(KD + k + 1) * P],
                            rden_wide[:, k * P:(k + 1) * P],
                            ident[:, :], start=True, stop=True), signal=filled[bank] if k == KD - 1 else None)
                    act.wait(filled[bank], f["aT_ready"])
                    act.do(lambda e, at: e.activation(ao[:, c % 2, :, :, :], banks[bank][:, :].rearrange(
                        "p (a k t) -> p a k t", a=2, k=KD), ACT.Copy), signal=drained[bank])
                    pool.wait(drained[bank], f["k_sq"])
                    pool.do(lambda e, at: e.tensor_tensor(
                        aT[:, :, c * P:(c + 1) * P], ao[:, c % 2, 0, :, :], ao[:, c % 2, 1, :, :],
                        ALU.mult), signal=f["aT_ready"])

            for n in range(len(work) + LAG + 1):
                if n > LAG:
                    values_of(n - LAG - 1)
                if n and n % PAIRS == 0:
                    c = n // PAIRS - 1
                    dve.wait(drained[(n - 1) % 2], f["rden_wide_ready"])
                    dve.do(lambda e, at, c=c: e.reciprocal(rden[:, :], den[:, c % 2, :]),
                           signal=f["rden_ready"])
                    pool.wait(f["rden_ready"], filled[3])
                    pool.do(lambda e, at: e.tensor_copy(
                        rden_wide[:, :].rearrange("p (h d) -> p h d", d=HD),
                        rden[:, :].rearrange("p (h o) -> p h o", o=1).broadcast_to([P, HEADS, HD])),
                        apart=True, signal=f["rden_wide_ready"])
                if LAG <= n < len(work) + LAG:
                    turn(n - LAG)
                if n < len(work):
                    scores_of(n)
                yield ATT

            pe.wait(f["aT_ready"])
            for n in range(GT // 2):
                bank = n
                product_rows(bank, n, lambda i, t: aT[:, i, t], lambda i: w_o[:, i, :], KD)
                dve.wait(filled[bank], f["ln_out"])
                dve.do(lambda e, at, n=n, bank=bank: e.tensor_tensor(
                    tiles(y, n), banks[bank][:, :], tiles(y, n), ALU.add), signal=drained[bank])
            yield 3
            dve.wait(drained[0], drained[1])
            pool.wait(drained[0], drained[1], f["ln_out"])
            pool.do(lambda e, at: e.tensor_tensor(x1[:, g, :, :], x_in[:, :, :], y[:, :, :], ALU.add),
                    signal=f["base_sum"])
            if prefetch is not None:
                sp.wait(f["base_sum"])
                sp.do(lambda e, at: e.dma_start(
                    x_in[:, :, :], x_view[bass.ds(at["round"] * GROUPS + prefetch, 1)].rearrange(
                        "o p t c -> (o p) t c")), signal=x_landed)
            pool.wait(f["base_sum"])
            pool.do(lambda e, at: e.tensor_tensor(
                x1[:, g, :, :], x1[:, g, :, :],
                b2_rows[:, :].rearrange("p (o c) -> p o c", o=1).broadcast_to([P, GT, D]), ALU.add),
                signal=f["base_ready"])
            normalize(y, z, drained[1])
            yield 8
            transposed(z, (0, 1), lambda c, bank: lambda e, at: e.activation(
                nT[:, c, 1:1 + G], bank[:, :], ACT.Identity, bias=col["ln2_b"][:, c:c + 1],
                scale=col["ln2_g"][:, c:c + 1]))
            yield 4
            pe.wait(drained[0], drained[1], w_back)
            for m in range(KF):
                bank = (2, 3, 0, 1)[m % 4]
                product_T(bank, lambda i, m=m: w_1[:, i, m * P:(m + 1) * P],
                          lambda i: nT[:, i, 1:1 + G], KD)
                act.wait(filled[bank])
                act.do(lambda e, at, m=m, bank=bank: e.activation(
                    hT[:, m, :], banks[bank][:, :], ACT.Gelu, bias=col["mlp_b1"][:, m:m + 1]),
                    signal=drained[bank])
                if m % 4 == 3:
                    yield 4
            pe.wait(*drained[0:4])
            for n in range(GT // 2):
                bank = n
                product_rows(bank, n, lambda i, t: hT[:, i, t], lambda i: w_2[:, i, :], KF)
                dve.wait(filled[bank], f["base_ready"])
                dve.do(lambda e, at, n=n, bank=bank: e.tensor_tensor(
                    tiles(x1[:, g, :, :], n), banks[bank][:, :], tiles(x1[:, g, :, :], n), ALU.add),
                    signal=drained[bank])
                yield 3.5

            normalize(x1[:, g, :, :], z, drained[1])
            dve.wait(f["diff_ready"], f["mix_ready"])
            if g == 0:
                dve.do(lambda e, at: e.memset(nT[:, :, 0:1], 0.0), signal=f["front_zero"])
            else:
                dve.do(lambda e, at: e.tensor_copy(nT[:, :, 0:1], last_n[:, :, :]), signal=f["front_zero"])
            yield 7
            transposed(z, (0, 1), lambda c, bank: lambda e, at: e.activation(
                nT[:, c, 1:1 + G], bank[:, :], ACT.Copy))
            pool.wait(drained[0], drained[1], f["front_zero"])
            pool.do(lambda e, at: e.tensor_tensor(diff, nT[:, :, 1:1 + G], nT[:, :, 0:G], ALU.subtract),
                    signal=f["diff_ready"])
            dve.wait(f["diff_ready"])
            if g == 0:
                dve.do(lambda e, at: e.tensor_copy(last_n[:, :, :], nT[:, :, G:G + 1]))
            for a, mu in ((1, "mu_k"), (0, "mu_r")):
                for k in range(KD):
                    dve.do(lambda e, at, a=a, mu=mu, k=k: e.scalar_tensor_tensor(
                        out=mixT[:, a, k, :], in0=diff[:, k, :], scalar=col[mu][:, k:k + 1],
                        in1=nT[:, k, 0:G], op0=ALU.mult, op1=ALU.add), signal=f["mix_ready"])
            yield 8
            pe.wait(but(2, f["mix_ready"]))
            for m in range(KD):
                bank = 2 + m
                product_T(bank, lambda i, m=m: w_k[:, i, m * P:(m + 1) * P],
                          lambda i: mixT[:, 1, i, :], KD)
                act.wait(filled[bank])
                act.do(lambda e, at, m=m, bank=bank: e.activation(
                    aT[:, m, :], banks[bank][:, :], ACT.Relu), signal=drained[bank])
                pool.wait(drained[bank])
                pool.do(lambda e, at, m=m: e.tensor_tensor(aT[:, m, :], aT[:, m, :], aT[:, m, :], ALU.mult),
                        signal=f["k_sq"])
            yield 2
            pe.wait(f["mix_ready"])
            for n in range(GT // 2):
                bank = n
                product_rows(bank, n, lambda i, t: mixT[:, 0, i, t], lambda i: w_r[:, i, :], KD)
                act.wait(filled[bank])
                act.do(lambda e, at, n=n, bank=bank: e.activation(
                    tiles(z, n), banks[bank][:, :], ACT.Tanh, scale=0.5), signal=drained[bank])
            yield 2
            pe.wait(f["k_sq"])
            for n in range(GT // 2):
                bank = 2 + n
                product_rows(bank, n, lambda i, t: aT[:, i, t], lambda i: w_v[:, i, :], KD)
                dve.wait(filled[bank], drained[0], drained[1])
                dve.do(lambda e, at, n=n, bank=bank: e.scalar_tensor_tensor(
                    out=tiles(z, n), in0=tiles(z, n), scalar=1.0, in1=banks[bank][:, :],
                    op0=ALU.add, op1=ALU.mult), signal=drained[bank])
            for n in range(GT // 2):
                dve.wait(drained[2 + n])
                dve.do(lambda e, at, n=n: e.scalar_tensor_tensor(
                    out=tiles(x1[:, g, :, :], n), in0=tiles(z, n), scalar=0.5,
                    in1=tiles(x1[:, g, :, :], n), op0=ALU.mult, op1=ALU.add), signal=f["x2_ready"])
            yield 3

        def middle(g):
            normalize(x1[:, g, :, :], z, f["x2_ready"])
            transposed(z, (0, 1), lambda c, bank: lambda e, at: e.activation(
                nT[:, c, 1:1 + G], bank[:, :], ACT.Copy))
            dve.wait(f["hc_used"], f["tail_ready"], f["hc_ready"])
            if g == 0:
                dve.do(lambda e, at: e.memset(xpT[:, :, 0:TAPS - 1], 0.0), signal=f["xp_ready"])
            else:
                dve.do(lambda e, at: e.tensor_copy(xpT[:, :, 0:TAPS - 1], xp_tail[:, :, :]),
                       signal=f["xp_ready"])
            pe.wait(drained[0], drained[1])
            for m in range(KE):
                bank = 2 + m
                product_T(bank, lambda i, m=m: w_in[:, i, m * P:(m + 1) * P],
                          lambda i: nT[:, i, 1:1 + G], KD)
                dve.wait(filled[bank], f["hc_ready"])
                dve.do(lambda e, at, m=m, bank=bank: e.tensor_copy(
                    xpT[:, m, TAPS - 1:TAPS - 1 + G], banks[bank][:, :]), signal=drained[bank])
            for m in range(KE):
                bank = (6, 7, 0, 1)[m]
                product_T(bank, lambda i, m=m: w_in[:, i, ED + m * P:ED + (m + 1) * P],
                          lambda i: nT[:, i, 1:1 + G], KD)
                act.wait(filled[bank], f["yg_ready"])
                act.do(lambda e, at, m=m, bank=bank: e.activation(
                    zs[:, m, :], banks[bank][:, :], ACT.Silu), signal=drained[bank])
            for m in range(KE):
                bank = 2 + m
                pe.wait(f["xp_ready"], drained[bank])
                product_T(bank, lambda i, m=m: conv_diag[:, m, i, :],
                          lambda i, m=m: xpT[:, m, i:i + G], TAPS)
                act.wait(filled[bank])
                act.do(lambda e, at, m=m, bank=bank: e.activation(
                    xc[:, m, :], banks[bank][:, :], ACT.Silu), signal=drained[bank])
            if g == 0:
                pool.wait(*drained[2:6])
                pool.do(lambda e, at: e.tensor_copy(xp_tail[:, :, :], xpT[:, :, G:G + TAPS - 1]),
                        apart=True, signal=f["tail_ready"])
            pe.wait(drained[2], drained[3], drained[4], drained[5])
            product_T(6, lambda i: w_x[:, i, :], lambda i: xc[:, i, :], KE, rows=RANK + 2 * NS)
            act.wait(filled[6], c_stored)
            act.do(lambda e, at: e.activation(dbc[:, :], banks[6][0:RANK + 2 * NS, :], ACT.Copy),
                   signal=drained[6])
            sp.wait(drained[6], *c_landed)
            sp.do(lambda e, at: e.dma_start(c_dram, dbc[RANK + NS:RANK + 2 * NS, :]), signal=c_stored)
            sp.wait(c_stored)
            load_c(0)
            pe.wait(drained[6])
            for m in range(KE):
                bank = 2 + m
                product_T(bank, lambda i, m=m: w_dt[:, m * P:(m + 1) * P], lambda i: dbc[0:RANK, :], 1)
                dve.wait(filled[bank])
                dve.do(lambda e, at, m=m, bank=bank: e.tensor_scalar(
                    delta[:, m, :], banks[bank][:, :], col["dt_b"][:, m:m + 1], 40.0, ALU.add, ALU.min),
                    signal=f["sp_in"])
            act.wait(f["sp_in"])
            act.do(lambda e, at: e.activation(delta[:, :, :], delta[:, :, :], ACT.Exp), signal=f["sp_exp"])
            act.wait(f["sp_exp"])
            for m in range(KE):
                act.do(lambda e, at, m=m: e.activation(delta[:, m, :], delta[:, m, :], ACT.Ln, bias=1.0),
                       signal=f["sp_ln"])
            for m in range(KE):
                bank = 2 + m
                dve.wait(but(KE - 1 - m, f["sp_ln"]))
                dve.do(lambda e, at, m=m, bank=bank: e.scalar_tensor_tensor(
                    out=delta[:, m, :], in0=banks[bank][:, :], scalar=col["dt_b"][:, m:m + 1],
                    in1=delta[:, m, :], op0=ALU.add, op1=ALU.max), signal=drained[bank])
            for m in range(KE):
                dve.wait(drained[2 + m])
                dve.do(lambda e, at, m=m: e.tensor_tensor(
                    u[:, m, :], delta[:, m, :], xc[:, m, :], ALU.mult), signal=f["u_ready"])

        def load_c(block):
            half, n0 = divmod(block, NS // CB)
            sp.wait(f["h_used"])
            sp.do(lambda e, at: e.dma_start(
                c_rows[:, block % 2, :, :],
                c_dram[n0 * CB:(n0 + 1) * CB, half * H:(half + 1) * H].rearrange(
                    "(o n) t -> o n t", o=1).broadcast_to([P, CB, H])), signal=c_landed[block % 2])

        def scan(g):
            steps = [(half, n, part) for half in range(2) for n in range(NS) for part in range(2)]

            def place(k):
                half, n, part = steps[k]
                return half, n, part, slice(2 * part, 2 * part + 2), slice(half * H, (half + 1) * H)

            def rows_b(i):
                half, n, _, _, ts = place(2 * i)
                bank = ROWS_B[i % 2]
                sel = ident[RANK:RANK + 2 * NS, RANK + n:RANK + n + 1].broadcast_to([2 * NS, P])
                pe.wait(drained[bank])
                pe.do(lambda e, at: e.matmul(banks[bank][:, 0:H], sel, dbc[RANK:RANK + 2 * NS, ts],
                                             start=True, stop=True), signal=filled[bank])

            def states_behind(k):
                return 0 if k < 2 or (g == GROUPS - 1 and k >= NS * 2) else 1

            def times_b(k):
                half, n, part, es, ts = place(k)
                bank = ROWS_B[k // 2 % 2]
                dve.wait(filled[bank], f["u_ready"], but(2 if k > 1 else 0, f["h_used"]),
                         but(states_behind(k), f["state_ready"]), f["tail_ready"])
                dve.do(lambda e, at: e.tensor_tensor(
                    bx[:, k // 2 % 2, es, :], u[:, es, ts],
                    banks[bank][:, 0:H].rearrange("p (o t) -> p o t", o=1).broadcast_to([P, 2, H]),
                    ALU.mult), signal=drained[bank] if part else f["bx_ready"])

            def decays(k):
                half, n, part, es, ts = place(k)
                act.wait(f["u_ready"], but(1 if k > 3 else 0, f["h_ready"]))
                for j in range(2):
                    act.do(lambda e, at, j=j: e.activation(
                        decay[:, k % RING, j, :], delta[:, 2 * part + j, ts], ACT.Exp,
                        scale=a_neg[:, 2 * part + j, n:n + 1]), signal=f["decay_ready"] if j else None)

            def run_h(k):
                half, n, part, es, ts = place(k)
                first = g == 0 and half == 0
                dve.wait(but(min(2, len(steps) - 1 - k), f["decay_ready"]), but(states_behind(k), f["state_ready"]))
                if part == 0 or k == len(steps) - 1:
                    dve.wait(f["bx_ready"], drained[ROWS_B[0]], drained[ROWS_B[1]])
                for j in range(2):
                    m = 2 * part + j
                    dve.do(lambda e, at, j=j, m=m: e.tensor_tensor_scan(
                        bx[:, k // 2 % 2, m, :], decay[:, k % RING, j, :], bx[:, k // 2 % 2, m, :],
                        0.0 if first else state[:, n, m:m + 1], ALU.mult, ALU.add),
                        signal=f["h_ready"] if j else None)

            def times_c(k):
                half, n, part, es, ts = place(k)
                i = k // 2
                pool.wait(f["h_ready"], f["hc_ready"], c_landed[i // CB % 2])
                if n % 2:
                    pool.wait(f["hc_used"])
                pool.do(lambda e, at: e.tensor_tensor(
                    hc[:, n % 2, es, :], bx[:, i % 2, es, :],
                    c_rows[:, (i // CB) % 2, i % CB:i % CB + 1, :].broadcast_to([P, 2, H]), ALU.mult),
                    signal=f["h_used"])
                if n % 2 and part:
                    pool.wait(f["h_used"])
                    for half_e in range(2):
                        es2 = slice(2 * half_e, 2 * half_e + 2)
                        pool.do(lambda e, at, es2=es2: e.tensor_tensor(
                            hc[:, 1, es2, :], hc[:, 0, es2, :], hc[:, 1, es2, :], ALU.add),
                            signal=f["hc_ready"])

            def keep_state(k):
                half, n, part, es, ts = place(k)
                if not (g == GROUPS - 1 and half == 1):
                    act.wait(f["h_ready"])
                    act.do(lambda e, at: e.activation(
                        state[:, n, es], bx[:, k // 2 % 2, es, H - 1], ACT.Copy), signal=f["state_ready"])

            def sum_n(n):
                pe.wait(f["hc_ready"])
                for part in range(2):
                    bank = Y[part]
                    if n == 1:
                        pe.wait(drained[bank])
                    pe.do(lambda e, at, part=part, bank=bank: e.matmul(
                        banks[bank][:, :], ident[:, :], flat(hc[:, 1, 2 * part:2 * part + 2, :]),
                        start=(n == 1), stop=(n == NS - 1)), signal=f["hc_used"])

            def gate(half):
                ts = slice(half * H, (half + 1) * H)
                for m in range(KE):
                    bank, j = Y[m // 2], m % 2
                    dve.wait(f["hc_used"])
                    dve.do(lambda e, at, m=m, bank=bank, j=j: e.scalar_tensor_tensor(
                        out=xc[:, m, ts], in0=xc[:, m, ts], scalar=col["D"][:, m:m + 1],
                        in1=banks[bank][:, j * H:(j + 1) * H], op0=ALU.mult, op1=ALU.add),
                        signal=drained[bank] if j else None)
                dve.wait(drained[Y[0]], drained[Y[1]], f["decay_ready"])
                dve.do(lambda e, at: e.tensor_tensor(
                    delta[:, :, ts], xc[:, :, ts], zs[:, :, ts], ALU.mult), signal=f["yg_ready"])

            pe.wait(drained[6])
            for i in range(2):
                rows_b(i)
            for k in range(2):
                decays(k)
            times_b(0)
            for k in range(len(steps) + 1):
                if k < len(steps):
                    if k % (2 * CB) == 0 and k // (2 * CB) + 1 < 2 * NS // CB:
                        load_c(k // (2 * CB) + 1)
                    if k + 2 < len(steps):
                        decays(k + 2)
                    if k + 1 < len(steps):
                        times_b(k + 1)
                    run_h(k)
                if k:
                    keep_state(k - 1)
                    if k % 4 == 0:
                        sum_n(k // 2 % NS - 1 if k // 2 % NS else NS - 1)
                if k < len(steps):
                    times_c(k)
                    if k % 2 == 0 and k and k // 2 + 1 < 2 * NS:
                        rows_b(k // 2 + 1)
                if k and k % (2 * NS) == 0:
                    gate(k // (2 * NS) - 1)
                yield 1.5

        def back(g):
            pe.wait(f["yg_ready"])
            for n in range(GT // 2):
                bank = n
                product_rows(bank, n, lambda i, t: delta[:, i, t], lambda i: w_out[:, i, :], KE)
                dve.wait(filled[bank], out_stored)
                dve.do(lambda e, at, n=n, bank=bank: e.tensor_tensor(
                    tiles(x3[:, g, :, :], n), banks[bank][:, :], tiles(x1[:, g, :, :], n), ALU.add),
                    signal=drained[bank])
            normalize(x3[:, g, :, :], z, drained[1])
            act.wait(f["mean_sum"])
            transposed(z, (2, 3), lambda c, bank: lambda e, at: e.activation(
                y4T[:, c, g * G:(g + 1) * G], bank[:, :], ACT.Copy, accum_out=sums[:, g, c:c + 1]))

        def route():
            dve.wait(drained[2], drained[3])
            dve.do(lambda e, at: e.tensor_tensor(mean[:, :], sums[:, 0, :], sums[:, 1, :], ALU.add),
                   signal=f["mean_sum"])
            dve.wait(f["mean_sum"])
            dve.do(lambda e, at: e.tensor_scalar(mean[:, :], mean[:, :], 1.0 / SEQ, None, ALU.mult),
                   signal=f["mean_ready"])
            pe.wait(f["mean_ready"], drained[0])
            for k in range(KD):
                pe.do(lambda e, at, k=k: e.matmul(banks[0][0:1, 0:EXPERTS], mean[:, k:k + 1],
                                                  w_route[:, k, :], start=(k == 0), stop=False))
            pe.do(lambda e, at: e.matmul(banks[0][0:1, 0:EXPERTS], ones_row[:, 0:1], b_route[:, :],
                                         start=False, stop=True), signal=filled[0])
            dve.wait(filled[0], f["pick_ready"])
            dve.do(lambda e, at: e.tensor_copy(scores[:, :], banks[0][0:1, 0:EXPERTS]), signal=drained[0])
            dve.wait(drained[0])
            dve.do(lambda e, at: e.max(top[:, :], scores[:, :]), apart=True, signal=f["max_ready"])
            dve.wait(f["max_ready"])
            dve.do(lambda e, at: e.max_index(top_i[:, :], top[:, :], scores[:, :]), apart=True,
                   signal=f["pick_ready"])
            sp.wait(f["pick_ready"])

            def load_expert(e, at):
                at["pick"] = e.value_load(top_i[0:1, 0:1], min_val=0, max_val=EXPERTS - 1)
                return e.dma_start(w_1[:, :, :], d["W1"][bass.ds(at["pick"], 1)].rearrange(
                    "e (k p) f -> p (e k) f", p=P))

            sp.do(load_expert, signal=w_picked)
            sp.do(lambda e, at: e.dma_start(w_2[:, :, :], d["W2"][bass.ds(at["pick"], 1)].rearrange(
                "e (k p) f -> p (e k) f", p=P)), signal=w_picked)
            sp.do(lambda e, at: e.dma_start(e_b1[:, :], d["b1"][bass.ds(at["pick"], 1)].rearrange(
                "e p k -> (e p) k")), signal=w_picked)
            sp.do(lambda e, at: e.dma_start(e_b2[:, :], d["b2"][bass.ds(at["pick"], 1)]),
                  signal=w_picked)

        def expert(more):
            pe.wait(w_picked, *drained)
            for g in range(GROUPS):
                for m in range(KM):
                    bank = 2 + m % 6
                    product_T(bank, lambda i, m=m: w_1[:, i, m * P:(m + 1) * P],
                              lambda i, g=g: y4T[:, i, g * G:(g + 1) * G], KD)
                    act.wait(filled[bank], w_picked)
                    act.do(lambda e, at, m=m, bank=bank: e.activation(
                        hT[:, m, :], banks[bank][:, :], ACT.Relu, bias=e_b1[:, m:m + 1]),
                        signal=drained[bank])
                pe.wait(*drained)
                for n in range(GT // 2):
                    bank = n
                    product_rows(bank, n, lambda i, t: hT[:, i, t], lambda i: w_2[:, i, :], KM,
                                 bias=e_b2[:, :])
                    dve.wait(filled[bank], f["ln_out"])
                    dve.do(lambda e, at, g=g, n=n, bank=bank: e.tensor_tensor(
                        tiles(x3[:, g, :, :], n), banks[bank][:, :], tiles(x3[:, g, :, :], n), ALU.add),
                        signal=drained[bank])
                sp.wait(drained[0], drained[1])
                sp.do(lambda e, at, g=g: e.dma_start(
                    out_view[bass.ds(at["round"] * GROUPS + g, 1)].rearrange("o p t c -> (o p) t c"),
                    x3[:, g, :, :]), signal=out_stored)
            if more:
                for dst, src in MLP_WEIGHTS:
                    sp.do(lambda e, at, dst=dst, src=src: e.dma_start(dst, src), signal=w_back)

        MLP_WEIGHTS = (
            (w_1[:, :, :], d["mlp_w1T"].rearrange("(k p) n -> p k n", p=P)),
            (w_2[:, :, :], d["mlp_w2T"].rearrange("(k p) n -> p k n", p=P)),
        )

        def alone(stream):
            for _ in stream:
                pass

        pg.part = "prologue"
        sp.do(lambda e, at: e.dma_start(x_in[:, :, :], x_view[0]), signal=x_landed)
        alone(front(0, 0, 1))
        middle(0)
        for part, last in (("body", False), ("epilogue", True)):
            pg.part = part
            interleave(front(0, 1, None if last else GROUPS), scan(0), FRONT_US, SCAN_US)
            back(0)
            middle(1)
            if last:
                alone(scan(1))
            else:
                interleave(front(1, 0, GROUPS + 1), scan(1), FRONT_US, SCAN_US)
            back(1)
            route()
            if not last:
                middle(0)
            expert(not last)

        block = ctx.enter_context(nc.Block())
        WEIGHTS = (
            (w_qkv[:, :, :], d["w_qkvT"].rearrange("(k p) n -> p k n", p=P)),
            (w_o[:, :, :], d["w_oT"].rearrange("(k p) n -> p k n", p=P)),
            (w_r[:, :, :], d["W_rT"].rearrange("(k p) n -> p k n", p=P)),
            (w_k[:, :, :], d["W_kT"].rearrange("(k p) n -> p k n", p=P)),
            (w_v[:, :, :], d["W_vT"].rearrange("(k p) n -> p k n", p=P)),
            (w_in[:, :, :], d["in_wT"].rearrange("(k p) n -> p k n", p=P)),
            (w_x[:, :, :], d["x_wT"].rearrange("(k p) n -> p k n", p=P)),
            (w_dt[:, :], d["dt_wT"]),
            (w_out[:, :, :], d["out_wT"].rearrange("(k p) n -> p k n", p=P)),
            (w_route[:, :, :], d["Wr"].rearrange("(k p) n -> p k n", p=P)),
            (b_route[:, :], d["br"]),
            (conv_w[:, :, :], d["conv_w"].rearrange("(k p) n -> p k n", p=P)),
            (a_neg[:, :, :], d["A_log"].rearrange("(k p) n -> p k n", p=P)),
            (b2_rows[:, :], d["mlp_b2"].broadcast_to([P, D])),
        ) + MLP_WEIGHTS + tuple((col[n], d[n]) for n in ("ln1_g", "ln1_b", "ln2_g", "ln2_b", "mlp_b1", "mu_r", "mu_k",
                                          "dt_b", "D"))

        def run(e, queue):
            queue.emit(e, "prologue", {"round": 0})
            with e.Fori(0, BATCH - 1) as i:
                queue.emit(e, "body", {"round": i})
            queue.emit(e, "epilogue", {"round": BATCH - 1, "rounds": BATCH - 1})

        def constants(e):
            e.wait_ge(s_w, 16 * len(WEIGHTS))
            e.wait_ge(s_pool, 1)
            e.wait_ge(s_dve, 3)
            e.wait_ge(s_diag, 1)
            e.wait_ge(s_act, 2)

        @block.sync
        def _(e):
            for fl in flags:
                e.sem_inc(fl.sem, CREDIT * fl.step)
            for dst, src in WEIGHTS:
                e.dma_start(dst, src).then_inc(s_w, 16)
            constants(e)
            run(e, sp)
            e.wait_ge(out_stored.sem, out_stored.step * (CREDIT + BATCH * GROUPS))

        @block.gpsimd
        def _(e):
            e.memset(ident[:, :], 0.0).then_inc(s_chain, 1)
            e.memset(band[:, :, :, :], 0.0).then_inc(s_chain, 1)
            e.memset(v_pad[:, :, :, :, :, :], 0.0)
            e.memset(spare[:, :], 0.0)
            e.memset(ones_row[:, :], 1.0)
            e.memset(power[:, :], -0.5)
            e.memset(kT[:, :, :], 0.0).then_inc(s_chain, 1)
            e.wait_ge(s_chain, 3)
            e.affine_select(out=ident[:, :], in_=ident[:, :], compare_op=ALU.not_equal, fill=1.0, base=0,
                            pattern=[[-1, P]], channel_multiplier=1).then_inc(s_chain, 1)
            e.affine_select(out=band[:, :, 0, :], in_=band[:, :, 0, :], compare_op=ALU.is_gt, fill=MASKED,
                            base=0, pattern=[[0, 2], [1, P]], channel_multiplier=-1).then_inc(s_chain, 1)
            e.affine_select(out=band[:, :, 1, :], in_=band[:, :, 1, :], compare_op=ALU.is_ge, fill=MASKED,
                            base=0, pattern=[[0, 2], [-1, P]], channel_multiplier=1).then_inc(s_chain, 1)
            e.wait_ge(s_chain, 6)
            e.tensor_copy(ident_bf[:, :], ident[:, :])
            e.tensor_copy(band_first[:, :, :, :], band[:, :, :, :]).then_inc(s_chain, 1)
            e.wait_ge(s_chain, 7)
            e.memset(band_first[:, :, 0, :], MASKED).then_inc(s_pool, 1)
            constants(e)
            run(e, pool)

        @block.vector
        def _(e):
            e.memset(col["even"], 0.0).then_inc(s_dve, 1)
            e.memset(scores[:, :], 0.0)
            e.wait_ge(s_dve, 1)
            for q in range(4):
                ins = e.memset(col["even"][32 * q:32 * q + 16, :], QSCALE)
            ins.then_inc(s_dve, 1)
            e.wait_ge(s_dve, 2)
            e.tensor_scalar(col["odd"], col["even"], -1.0, QSCALE, ALU.mult, ALU.add).then_inc(s_dve, 1)
            e.wait_ge(s_w, 16 * len(WEIGHTS))
            e.wait_ge(s_pool, 1)
            for m in range(KE):
                for k in range(TAPS):
                    ins = e.tensor_scalar(conv_diag[:, m, k, :], ident[:, :], conv_w[:, m, k:k + 1], None,
                                          ALU.mult)
            ins.then_inc(s_diag, 1)
            constants(e)
            run(e, dve)

        @block.scalar
        def _(e):
            e.wait_ge(s_w, 16 * len(WEIGHTS))
            e.activation(a_neg[:, :, :], a_neg[:, :, :], ACT.Exp).then_inc(s_act, 1)
            e.wait_ge(s_act, 1)
            e.activation(a_neg[:, :, :], a_neg[:, :, :], ACT.Copy, scale=-1.0).then_inc(s_act, 1)
            constants(e)
            run(e, act)

        @block.tensor
        def _(e):
            constants(e)
            run(e, pe)


def kernel(**inputs):
    import numpy as np
    import concourse.bacc as bacc
    from concourse.bass_utils import run_bass_kernel_spmd

    a = {n: np.asarray(v) for n, v in inputs.items()}

    def columns(v):
        return np.ascontiguousarray(v.reshape(-1, P).T)

    def transposed(v):
        return np.ascontiguousarray(v.T)

    arrays = {
        "x": a["L0_attn_x"],
        "w_qkvT": transposed(a["L0_attn_w_qkv"]), "w_oT": transposed(a["L0_attn_w_o"]),
        "ln1_g": columns(a["L0_attn_ln1_g"]), "ln1_b": columns(a["L0_attn_ln1_b"]),
        "ln2_g": columns(a["L0_attn_ln2_g"]), "ln2_b": columns(a["L0_attn_ln2_b"]),
        "mlp_w1T": transposed(a["L0_attn_mlp_w1"]), "mlp_b1": columns(a["L0_attn_mlp_b1"]),
        "mlp_w2T": transposed(a["L0_attn_mlp_w2"]), "mlp_b2": a["L0_attn_mlp_b2"].reshape(1, -1),
        "W_rT": transposed(a["L0_ffn_W_r"]), "W_kT": transposed(a["L0_ffn_W_k"]),
        "W_vT": transposed(a["L0_ffn_W_v"]),
        "mu_r": columns(a["L0_ffn_mu_r"]), "mu_k": columns(a["L0_ffn_mu_k"]),
        "in_wT": transposed(a["L1_attn_in_proj_w"]),
        "conv_w": a["L1_attn_conv_w"].reshape(a["L1_attn_conv_w"].shape[0], -1),
        "x_wT": transposed(a["L1_attn_x_proj_w"]), "dt_wT": transposed(a["L1_attn_dt_proj_w"]),
        "dt_b": columns(a["L1_attn_dt_proj_b"]), "A_log": a["L1_attn_A_log"],
        "D": columns(a["L1_attn_D"]), "out_wT": transposed(a["L1_attn_out_proj_w"]),
        "Wr": a["L1_ffn_Wr"], "br": a["L1_ffn_br"].reshape(1, -1),
        "W1": a["L1_ffn_W1"],
        "b1": np.ascontiguousarray(a["L1_ffn_b1"].reshape(a["L1_ffn_b1"].shape[0], -1, P).transpose(0, 2, 1)),
        "W2": a["L1_ffn_W2"], "b2": a["L1_ffn_b2"],
    }
    nc = bacc.Bacc("TRN2", target_bir_lowering=False, num_devices=1)
    d = {n: nc.dram_tensor(f"in_{n}", v.shape, mybir.dt.from_np(v.dtype), kind="ExternalInput").ap()
         for n, v in arrays.items()}
    x = arrays["x"]
    d["out"] = nc.dram_tensor("out_y", x.shape, mybir.dt.from_np(x.dtype), kind="ExternalOutput").ap()
    build_block_stack(nc, d)
    r = run_bass_kernel_spmd(nc, [{f"in_{n}": v for n, v in arrays.items()}], core_ids=[0])
    return r.results[0]["out_y"]
```

```python
from contextlib import ExitStack

import concourse.bass as bass
from concourse import mybir

ALU = mybir.AluOpType
ACT = mybir.ActivationFunctionType
AX = mybir.AxisListType
F32 = mybir.dt.float32
BF16 = mybir.dt.bfloat16
U32 = mybir.dt.uint32

P = 128


CREDIT = 4


class Flag:

    def __init__(self, nc, ctx, name, step=1):
        self.sem = ctx.enter_context(nc.semaphore(name))
        self.step = step
        self.count = {"prologue": 0, "body": 0, "epilogue": 0}

    def value(self, place, at):
        part, k = place
        k += CREDIT
        if part != "prologue":
            k += self.count["prologue"]
        if part == "epilogue":
            k += self.count["body"] * at["rounds"]
        if part == "body":
            return (at["round"] * self.count["body"] + k) * self.step
        return k * self.step


def but(n, flag):
    return flag, n


class Queue:

    def __init__(self, program, passed, hold_each=False):
        self.program = program
        self.passed = passed
        self.hold_each = hold_each
        self.items = {"prologue": [], "body": [], "epilogue": []}

    def wait(self, *flags):
        part = self.program.part
        for f in flags:
            f, back = f if isinstance(f, tuple) else (f, 0)
            self.items[part].append(("wait", f, (part, f.count[part] - back)))

    def do(self, fn, signal=None, apart=False):
        part = self.program.part
        if apart and self.items[part] and self.items[part][-1][0] == "wait":
            self.items[part].append(("hold", None, None))
        self.items[part].append(("do", fn, signal))
        if signal is not None:
            signal.count[part] += 1

    def emit(self, eng, part, at):
        waited = {}
        for kind, a, b in self.items[part]:
            if kind == "wait":
                if waited.get(id(a), -99) < b[1]:
                    eng.wait_ge(a.sem, a.value(b, at))
                    waited[id(a)] = b[1]
                    if self.hold_each:
                        eng.sem_inc(self.passed, 1)
            elif kind == "hold":
                eng.sem_inc(self.passed, 1)
            else:
                ins = a(eng, at)
                if b is not None:
                    ins.then_inc(b.sem, b.step)


class Program:
    def __init__(self, passed):
        self.part = "prologue"
        self.pe, self.act, self.dve, self.pool = (Queue(self, passed[n]) for n in range(4))
        self.sp = Queue(self, passed[4], hold_each=True)


def interleave(long, short, long_cost, short_cost):
    done_long = done_short = 0.0
    short_left = short is not None
    for cost in long:
        done_long += cost
        while short_left and done_short / short_cost < done_long / long_cost:
            c = next(short, None)
            if c is None:
                short_left = False
            else:
                done_short += c
    if short_left:
        for _ in short:
            pass


def build_block_stack(nc, d):
    BATCH, SEQ, D = d["x"].shape
    KD = D // P
    GT = 4
    G = GT * P
    GROUPS = SEQ // G
    HEADS, HD = 16, 16
    WINDOW = 128
    FF = d["mlp_w1T"].shape[1]
    KF = FF // P
    ED = d["out_wT"].shape[0]
    KE = ED // P
    NS = d["A_log"].shape[1]
    RANK = d["dt_wT"].shape[0]
    TAPS = d["conv_w"].shape[1]
    EXPERTS, _, MFF = d["W1"].shape
    KM = MFF // P
    EPS = 1e-5
    MASKED = -1e30
    QSCALE = float(HD) ** -0.5
    PAIRS = HEADS // 2
    H = G // 2
    CB = 4
    RING, LAG = 4, 2
    ATT = 2.2
    MIDDLE_COST, BACK_COST, TAIL_COST = 42.0, 30.0, 60.0
    SUM_AT = 3
    FRONT_COST, SCAN_COST = 138.0, 96.0
    assert WINDOW == P and SEQ % G == 0 and HD == 16

    with ExitStack() as ctx:
        def sb(name, shape, dt=F32):
            return ctx.enter_context(nc.sbuf_tensor(name, shape, dt))

        def flag(name, step=1):
            f = Flag(nc, ctx, name, step)
            flags.append(f)
            return f

        flags = []
        banks = [ctx.enter_context(nc.psum_tensor(f"bank{i}", [P, 512], F32)) for i in range(8)]
        filled = [flag(f"filled{i}") for i in range(8)]
        drained = [flag(f"drained{i}") for i in range(8)]

        w_qkv = sb("w_qkv", [P, KD, 3 * D])
        w_o = sb("w_o", [P, KD, D])
        w_1 = sb("w_1", [P, KD, FF])
        w_2 = sb("w_2", [P, KF, D])
        w_r = sb("w_r", [P, KD, D])
        w_k = sb("w_k", [P, KD, D])
        w_v = sb("w_v", [P, KD, D])
        w_in = sb("w_in", [P, KD, 2 * ED])
        w_x = sb("w_x", [P, KE, RANK + 2 * NS])
        w_dt = sb("w_dt", [RANK, ED])
        w_out = sb("w_out", [P, KE, D])
        w_route = sb("w_route", [P, KD, EXPERTS])
        b_route = sb("b_route", [1, EXPERTS])
        vecs = sb("vecs", [P, 64])
        conv_w = sb("conv_w", [P, KE, TAPS])
        conv_diag = sb("conv_diag", [P, KE, TAPS, P])
        a_neg = sb("a_neg", [P, KE, NS])
        b2_rows = sb("b2_rows", [P, D])
        ident = sb("ident", [P, P])
        ident_bf = sb("ident_bf", [P, P], BF16)
        band = sb("band", [P, 2, 2, P], BF16)
        band_first = sb("band_first", [P, 2, 2, P], BF16)
        ones_row = sb("ones_row", [1, P])
        power = sb("power", [P, GT])

        col = {}
        at_col = 0
        for name, n in (("ln1_g", KD), ("ln1_b", KD), ("ln2_g", KD), ("ln2_b", KD), ("mlp_b1", KF),
                        ("mu_r", KD), ("mu_k", KD), ("dt_b", KE), ("D", KE),
                        ("own", 8)):
            col[name] = vecs[:, at_col:at_col + n]
            at_col += n
        assert at_col <= 64

        x_in = sb("x_in", [P, GT, D])
        y = sb("y", [P, GT, D])
        z = sb("z", [P, GT, D])
        ao = z[:, :, :].rearrange("p t c -> p (t c)").rearrange("p (r a k t) -> p r a k t", r=2, a=2, k=KD)
        x1 = sb("x1", [P, GROUPS, GT, D])
        stats = sb("stats", [P, GT, 6])
        mean_var = sb("mean_var", [P, GT, 2])
        rstd = sb("rstd", [P, GT])
        nT = sb("nT", [P, KD, 1 + G])
        last_n = sb("last_n", [P, KD, 1])
        kT = sb("kT", [P, KD, WINDOW + G])
        v_pad = sb("v_pad", [P, 1 + GT, PAIRS, 2, 2, HD])
        neg_max = sb("neg_max", [P, HEADS])
        den = sb("den", [P, 2, HEADS])
        rden = sb("rden", [P, HEADS])
        rden_wide = sb("rden_wide", [P, D])
        aT = sb("aT", [P, KD, G])
        probT = sb("probT", [P, 2, 2, 2 * P])
        region_f = sb("region_f", [P, KF * G])
        q_own = region_f[:, 0:2048].rearrange("p (r h t) -> p r h t", r=2, h=8)
        prob = region_f[:, 2048:4096].rearrange("p (r a k) -> p r a k", r=RING, a=2)
        hT = region_f[:, 0:KF * G].rearrange("p (f t) -> p f t", t=G)
        mixT = region_f[:, 0:4 * G].rearrange("p (a k t) -> p a k t", a=2, k=KD)
        diff = region_f[:, 4 * G:6 * G].rearrange("p (k t) -> p k t", k=KD)
        xp_tail = sb("xp_tail", [P, KE, TAPS - 1])
        zs = sb("zs", [P, KE, G])
        xc = sb("xc", [P, KE, G])
        dbc = sb("dbc", [RANK + 2 * NS, G])
        delta = sb("delta", [P, KE, G])
        u = sb("u", [P, KE, G])
        state = sb("state", [P, NS, KE])
        region_s = sb("region_s", [P, 4 * KE * H])
        bx = region_s[:, 0:2 * KE * H].rearrange("p (r e t) -> p r e t", r=2, e=KE)
        hc = region_s[:, 2 * KE * H:4 * KE * H].rearrange("p (r e t) -> p r e t", r=2, e=KE)
        xpT = region_s[:, 0:KE * (TAPS - 1 + G)].rearrange("p (e t) -> p e t", e=KE)
        c_rows = sb("c_rows", [P, 2, CB, H])
        decay = sb("decay", [P, RING, 2, H])
        x3 = sb("x3", [P, GROUPS, GT, D])
        y4T = sb("y4T", [P, KD, SEQ])
        sums = sb("sums", [P, GROUPS, KD])
        mean = sb("mean", [P, KD])
        scores = sb("scores", [1, 8])
        top = sb("top", [1, 8])
        top_i = sb("top_i", [1, 8], U32)
        e_b1 = sb("e_b1", [P, KM])
        e_b2 = sb("e_b2", [1, D])
        c_dram = nc.dram_tensor("c_rows_dram", (NS, G), F32, kind="Internal").ap()

        s_w = ctx.enter_context(nc.semaphore("weights_landed"))
        s_pool = ctx.enter_context(nc.semaphore("gpsimd_constants"))
        s_diag = ctx.enter_context(nc.semaphore("conv_diag_built"))
        s_act = ctx.enter_context(nc.semaphore("a_neg_built"))
        s_chain = ctx.enter_context(nc.semaphore("constants_step"))
        s_dve = ctx.enter_context(nc.semaphore("vector_constants"))

        x_landed = flag("x_landed", 16)
        c_stored = flag("c_stored", 16)
        c_landed = [flag(f"c_landed{i}", 16) for i in range(2)]
        w_picked = flag("w_picked", 16)
        w_back = flag("w_back", 16)
        out_stored = flag("out_stored", 16)
        f = {n: flag(n) for n in (
            "ln_stats", "ln_rstd", "ln_out", "carry_in", "neg_max_ready", "q_own_ready", "rden_ready",
            "rden_wide_ready", "aT_ready", "base_sum", "base_ready", "front_zero", "diff_ready",
            "mix_ready", "k_sq", "x2_ready", "xp_ready", "tail_ready", "sp_in", "sp_exp", "sp_ln",
            "u_ready", "bx_ready", "h_used", "decay_ready", "h_ready", "hc_ready", "hc_used",
            "state_ready", "yg_ready", "mean_sum", "mean_ready", "max_ready", "pick_ready")}

        pg = Program([ctx.enter_context(nc.semaphore(f"held{n}")) for n in range(5)])
        pe, act, dve, pool, sp = pg.pe, pg.act, pg.dve, pg.pool, pg.sp

        x_view = d["x"].rearrange("b (g t p) c -> (b g) p t c", g=GROUPS, p=P)
        out_view = d["out"].rearrange("b (g t p) c -> (b g) p t c", g=GROUPS, p=P)

        def flat(ap):
            return ap.rearrange("p t c -> p (t c)")


        def normalize(src, dst, ready, free=(), readers=(0, 1, 2, 3)):
            dve.wait(ready, f["ln_stats"], f["ln_rstd"])
            for t in range(GT):
                dve.do(lambda e, at, t=t: e.bn_stats(stats[:, t, :], src[:, t, :]),
                       signal=f["ln_stats"] if t == GT - 1 else None)
            dve.wait(f["ln_stats"])
            for t in range(GT):
                dve.do(lambda e, at, t=t: e.bn_aggr(mean_var[:, t, :], stats[:, t, :]), apart=True,
                       signal=f["ln_stats"] if t == GT - 1 else None)
            pool.wait(f["ln_stats"], f["ln_out"])
            pool.do(lambda e, at: e.tensor_scalar(rstd[:, :], mean_var[:, :, 1], EPS, None, ALU.add),
                    apart=True, signal=f["ln_rstd"])
            pool.wait(f["ln_rstd"])
            pool.do(lambda e, at: e.tensor_tensor(rstd[:, :], rstd[:, :], power[:, :], ALU.pow),
                    signal=f["ln_rstd"])
            yield 3
            dve.wait(f["ln_rstd"], *(filled[b] for b in readers), *free)
            for t in range(GT):
                dve.do(lambda e, at, t=t: e.tensor_scalar(
                    dst[:, t, :], src[:, t, :], mean_var[:, t, 0:1], rstd[:, t:t + 1],
                    ALU.subtract, ALU.mult), signal=f["ln_out"] if t == GT - 1 else None)

        def transposed(src, pair, evacuate):
            pe.wait(f["ln_out"])
            for c in range(KD):
                bank = pair[c]
                pe.wait(drained[bank])
                for t in range(GT):
                    pe.do(lambda e, at, t=t, c=c, bank=bank: e.transpose(
                        banks[bank][:, t * P:(t + 1) * P], src[:, t, c * P:(c + 1) * P], ident[:, :]),
                        signal=filled[bank] if t == GT - 1 else None)
            for c in range(KD):
                act.wait(filled[pair[c]])
                act.do(evacuate(c, banks[pair[c]]), signal=drained[pair[c]])

        def product_T(bank, lhsT, rhs, parts, rows=P):
            pe.wait(drained[bank])
            for i in range(parts):
                pe.do(lambda e, at, i=i: e.matmul(banks[bank][0:rows, :], lhsT(i), rhs(i),
                                                  start=(i == 0), stop=(i == parts - 1)),
                      signal=filled[bank] if i == parts - 1 else None)

        def product_rows(bank, n, srcT, weight, parts, bias=None):
            pe.wait(drained[bank])
            for j in range(2):
                t = 2 * n + j
                for i in range(parts):
                    pe.do(lambda e, at, i=i, j=j, t=t: e.matmul(
                        banks[bank][:, j * D:(j + 1) * D], srcT(i, slice(t * P, (t + 1) * P)), weight(i),
                        start=(i == 0), stop=(i == parts - 1 and bias is None)),
                        signal=filled[bank] if (j == 1 and i == parts - 1 and bias is None) else None)
                if bias is not None:
                    pe.do(lambda e, at, j=j: e.matmul(
                        banks[bank][:, j * D:(j + 1) * D], ones_row[:, :], bias, start=False, stop=True),
                        signal=filled[bank] if j == 1 else None)

        def tiles(t, n):
            return flat(t[:, 2 * n:2 * n + 2, :])

        ROWS_B, Y = (4, 5), (6, 7)
        LOW, DT = 2, (3, 0, 1, 6)
        TAIL = (4, 5)


        def head():
            yield from normalize(x_in, y, x_landed, [f["base_ready"]])
            yield 3
            yield from normalize(y, z, f["ln_out"], [f["x2_ready"]], range(6))
            yield 3

        def front(s, g, prefetch):
            qT = x1[:, g, :, :].rearrange("p t c -> p (t c)").rearrange("p (k t) -> p k t", k=KD)
            transposed(z, (0, 1), lambda c, bank: lambda e, at: e.activation(
                nT[:, c, 1:1 + G], bank[:, :], ACT.Identity, bias=col["ln1_b"][:, c:c + 1],
                scale=col["ln1_g"][:, c:c + 1]))
            pool.wait(*filled[0:4], drained[3])
            if g == 0:
                pool.do(lambda e, at: e.memset(kT[:, :, 0:WINDOW], 0.0), apart=True)
                pool.do(lambda e, at: e.memset(v_pad[:, 0, :, :, :, :], 0.0), signal=f["carry_in"])
            else:
                pool.do(lambda e, at: e.tensor_copy(kT[:, :, 0:WINDOW], kT[:, :, G:G + WINDOW]), apart=True)
                pool.do(lambda e, at: e.tensor_copy(v_pad[:, 0, :, :, :, :], v_pad[:, GT, :, :, :, :]),
                        signal=f["carry_in"])
            yield 4
            pe.wait(drained[0], drained[1])
            for m in range(2 * KD):
                bank = (2, 3, 0, 1)[m]
                product_T(bank, lambda i, m=m: w_qkv[:, i, m * P:(m + 1) * P],
                          lambda i: nT[:, i, 1:1 + G], KD)
                if m < KD:
                    act.wait(filled[bank], f["x2_ready"], *(drained[0:4] if m == 0 else ()))
                    act.do(lambda e, at, m=m, bank=bank: e.activation(
                        qT[:, m, :], banks[bank][:, :], ACT.Copy, scale=QSCALE), signal=drained[bank])
                else:
                    dve.wait(filled[bank], f["carry_in"])
                    dve.do(lambda e, at, m=m, bank=bank: e.tensor_copy(
                        kT[:, m - KD, WINDOW:WINDOW + G], banks[bank][:, :]), signal=drained[bank])
                yield 1
            for n in range(GT // 2):
                bank = 2 + n
                product_rows(bank, n, lambda i, t: nT[:, i, 1 + t.start:1 + t.stop],
                             lambda i: w_qkv[:, i, 2 * D:3 * D], KD)
                dve.wait(filled[bank], f["carry_in"])
                for par in range(2):
                    dve.do(lambda e, at, n=n, par=par, bank=bank: e.tensor_copy(
                        v_pad[:, 1 + 2 * n:3 + 2 * n, :, par, par, :],
                        banks[bank][:, :].rearrange("p (t a b d) -> p t a b d", t=2, b=2, d=HD)[:, :, :, par, :]),
                        signal=drained[bank] if par else None)
                yield 1.5
            def own_channels(c, k):
                pool.wait(filled[0], filled[1], drained[2 + k])
                pool.do(lambda e, at: e.tensor_tensor(
                    q_own[:, k, :, :],
                    qT[:, k:k + 1, c * P:(c + 1) * P].broadcast_to([P, 8, P]),
                    col["own"].rearrange("p (h o) -> p h o", o=1).broadcast_to([P, 8, P]), ALU.mult),
                    signal=f["q_own_ready"])

            work = [(c, p) for c in range(GT) for p in range(PAIRS)]
            pe.wait(*drained[0:4])

            def scores_of(n):
                c, p = work[n]
                bank = n % 2
                k = p // 4
                if p % 4 == 0:
                    pe.wait(f["q_own_ready"])
                mask = band_first if (g == 0 and c == 0) else band
                pe.wait(drained[bank])
                pe.do(lambda e, at: e.matmul(banks[bank][:, :], ident_bf[:, :],
                                             mask[:, :, :, :].rearrange("p a b k -> p (a b k)"),
                                             start=True, stop=False, skip_group_check=True))
                for par in range(2):
                    pe.do(lambda e, at, par=par: e.matmul(
                        banks[bank][:, 256 * par:256 * par + 256],
                        q_own[:, k, 2 * (p % 4) + par, :], kT[:, k, c * P:(c + 2) * P],
                        start=False, stop=(par == 1), skip_group_check=True),
                        signal=filled[bank] if par == 1 else None)

            def weights_of(n):
                c, p = work[n]
                bank, r = n % 2, n % RING
                dve.wait(filled[bank])
                dve.do(lambda e, at: e.tensor_reduce(
                    neg_max[:, 2 * p:2 * p + 2], banks[bank][:, :].rearrange("p (a k) -> p a k", a=2),
                    AX.X, ALU.max, negate=True), signal=f["neg_max_ready"])
                act.wait(f["neg_max_ready"], but(RING - LAG, filled[2]))
                for par in range(2):
                    h = 2 * p + par
                    act.do(lambda e, at, par=par, h=h: e.activation(
                        prob[:, r, par, :], banks[bank][:, 256 * par:256 * par + 256], ACT.Exp,
                        bias=neg_max[:, h:h + 1], accum_out=den[:, c % 2, h:h + 1]),
                        signal=drained[bank] if par else None)

            def turn(n):
                bank, r = 2, n % RING
                pe.wait(drained[bank], drained[n % 2])
                for par in range(2):
                    for half in range(2):
                        pe.do(lambda e, at, par=par, half=half: e.transpose(
                            banks[bank][:, (2 * par + half) * P:(2 * par + half + 1) * P],
                            prob[:, r, par, half * P:(half + 1) * P], ident[:, :]),
                            signal=filled[bank] if par and half else None)
                act.wait(filled[bank])
                act.do(lambda e, at: e.activation(
                    flat(probT[:, n % 2, :, :]), banks[bank][:, :], ACT.Copy), signal=drained[bank])

            def values_of(n):
                c, p = work[n]
                bank = 3
                k, q = divmod(p, 4)
                if p == 0:
                    pe.wait(drained[bank])
                pe.wait(drained[2])
                for i, (par, half) in enumerate(((0, 0), (0, 1), (1, 0), (1, 1))):
                    pe.do(lambda e, at, i=i, par=par, half=half: e.matmul(
                        banks[bank][32 * q:32 * q + 32, k * P:(k + 1) * P],
                        v_pad[:, c + half, p, par, :, :].rearrange("p b d -> p (b d)"),
                        probT[:, n % 2, par, half * P:(half + 1) * P],
                        start=(i == 0), stop=(i == 3)))
                if p == PAIRS - 1:
                    pe.wait(f["rden_wide_ready"])
                    for k in range(KD):
                        pe.do(lambda e, at, k=k: e.matmul(
                            banks[bank][:, (KD + k) * P:(KD + k + 1) * P],
                            rden_wide[:, k * P:(k + 1) * P],
                            ident[:, :], start=True, stop=True), signal=filled[bank] if k == KD - 1 else None)
                    act.wait(filled[bank], f["aT_ready"])
                    act.do(lambda e, at: e.activation(ao[:, c % 2, :, :, :], banks[bank][:, :].rearrange(
                        "p (a k t) -> p a k t", a=2, k=KD), ACT.Copy), signal=drained[bank])
                    pool.wait(drained[bank], f["k_sq"])
                    pool.do(lambda e, at: e.tensor_tensor(
                        aT[:, :, c * P:(c + 1) * P], ao[:, c % 2, 0, :, :], ao[:, c % 2, 1, :, :],
                        ALU.mult), signal=f["aT_ready"])

            own_channels(0, 0)
            for n in range(len(work) + LAG + 1):
                if n < len(work):
                    scores_of(n)
                if n > LAG:
                    values_of(n - LAG - 1)
                if n and n % PAIRS == 0:
                    c = n // PAIRS - 1
                    dve.wait(drained[(n - 1) % 2], f["rden_wide_ready"])
                    dve.do(lambda e, at, c=c: e.reciprocal(rden[:, :], den[:, c % 2, :]),
                           signal=f["rden_ready"])
                    pool.wait(f["rden_ready"], filled[3])
                    pool.do(lambda e, at: e.tensor_copy(
                        rden_wide[:, :].rearrange("p (h d) -> p h d", d=HD),
                        rden[:, :].rearrange("p (h o) -> p h o", o=1).broadcast_to([P, HEADS, HD])),
                        apart=True, signal=f["rden_wide_ready"])
                if LAG <= n < len(work) + LAG:
                    turn(n - LAG)
                if n < len(work):
                    weights_of(n)
                if n % 4 == 0 and n + 4 < len(work):
                    c, p = work[n + 4]
                    own_channels(c, p // 4)
                yield ATT

            pe.wait(f["aT_ready"])
            for n in range(GT // 2):
                bank = n
                product_rows(bank, n, lambda i, t: aT[:, i, t], lambda i: w_o[:, i, :], KD)
                dve.wait(filled[bank], f["ln_out"])
                dve.do(lambda e, at, n=n, bank=bank: e.tensor_tensor(
                    tiles(y, n), banks[bank][:, :], tiles(y, n), ALU.add), signal=drained[bank])
            yield 3
            dve.wait(drained[0], drained[1])
            ln = normalize(y, z, drained[1])
            yield next(ln)
            pool.wait(drained[1])
            pool.do(lambda e, at: e.tensor_tensor(x1[:, g, :, :], x_in[:, :, :], y[:, :, :], ALU.add),
                    signal=f["base_sum"])
            if prefetch is not None:
                sp.wait(f["base_sum"])
                sp.do(lambda e, at: e.dma_start(
                    x_in[:, :, :], x_view[bass.ds(at["round"] * GROUPS + prefetch, 1)].rearrange(
                        "o p t c -> (o p) t c")), signal=x_landed)
            pool.wait(f["base_sum"])
            pool.do(lambda e, at: e.tensor_tensor(
                x1[:, g, :, :], x1[:, g, :, :],
                b2_rows[:, :].rearrange("p (o c) -> p o c", o=1).broadcast_to([P, GT, D]), ALU.add),
                signal=f["base_ready"])
            yield from ln
            yield 3
            transposed(z, (0, 1), lambda c, bank: lambda e, at: e.activation(
                nT[:, c, 1:1 + G], bank[:, :], ACT.Identity, bias=col["ln2_b"][:, c:c + 1],
                scale=col["ln2_g"][:, c:c + 1]))
            yield 4
            pe.wait(drained[0], drained[1], w_back)
            for m in range(KF):
                bank = (2, 3, 0, 1)[m % 4]
                product_T(bank, lambda i, m=m: w_1[:, i, m * P:(m + 1) * P],
                          lambda i: nT[:, i, 1:1 + G], KD)
                act.wait(filled[bank])
                act.do(lambda e, at, m=m, bank=bank: e.activation(
                    hT[:, m, :], banks[bank][:, :], ACT.Gelu, bias=col["mlp_b1"][:, m:m + 1]),
                    signal=drained[bank])
                if m % 4 == 3:
                    yield 4
            pe.wait(*drained[0:4])
            for n in range(GT // 2):
                bank = n
                product_rows(bank, n, lambda i, t: hT[:, i, t], lambda i: w_2[:, i, :], KF)
                dve.wait(filled[bank], f["base_ready"])
                dve.do(lambda e, at, n=n, bank=bank: e.tensor_tensor(
                    tiles(x1[:, g, :, :], n), banks[bank][:, :], tiles(x1[:, g, :, :], n), ALU.add),
                    signal=drained[bank])
                yield 3.5

            yield from normalize(x1[:, g, :, :], z, drained[1])
            dve.wait(f["diff_ready"], f["mix_ready"])
            if g == 0:
                dve.do(lambda e, at: e.memset(nT[:, :, 0:1], 0.0), signal=f["front_zero"])
            else:
                dve.do(lambda e, at: e.tensor_copy(nT[:, :, 0:1], last_n[:, :, :]), signal=f["front_zero"])
            yield 4
            transposed(z, (0, 1), lambda c, bank: lambda e, at: e.activation(
                nT[:, c, 1:1 + G], bank[:, :], ACT.Copy))
            pool.wait(drained[0], drained[1], f["front_zero"])
            pool.do(lambda e, at: e.tensor_tensor(diff, nT[:, :, 1:1 + G], nT[:, :, 0:G], ALU.subtract),
                    signal=f["diff_ready"])
            dve.wait(f["diff_ready"])
            if g == 0:
                dve.do(lambda e, at: e.tensor_copy(last_n[:, :, :], nT[:, :, G:G + 1]))
            for a, mu in ((1, "mu_k"), (0, "mu_r")):
                for k in range(KD):
                    dve.do(lambda e, at, a=a, mu=mu, k=k: e.scalar_tensor_tensor(
                        out=mixT[:, a, k, :], in0=diff[:, k, :], scalar=col[mu][:, k:k + 1],
                        in1=nT[:, k, 0:G], op0=ALU.mult, op1=ALU.add), signal=f["mix_ready"])
            yield 10
            pe.wait(but(2, f["mix_ready"]))
            for m in range(KD):
                bank = 2 + m
                product_T(bank, lambda i, m=m: w_k[:, i, m * P:(m + 1) * P],
                          lambda i: mixT[:, 1, i, :], KD)
                act.wait(filled[bank])
                act.do(lambda e, at, m=m, bank=bank: e.activation(
                    aT[:, m, :], banks[bank][:, :], ACT.Relu), signal=drained[bank])
                pool.wait(drained[bank])
                pool.do(lambda e, at, m=m: e.tensor_tensor(aT[:, m, :], aT[:, m, :], aT[:, m, :], ALU.mult),
                        signal=f["k_sq"])
            yield 2
            pe.wait(f["mix_ready"])
            for n in range(GT // 2):
                bank = n
                product_rows(bank, n, lambda i, t: mixT[:, 0, i, t], lambda i: w_r[:, i, :], KD)
                act.wait(filled[bank])
                act.do(lambda e, at, n=n, bank=bank: e.activation(
                    tiles(z, n), banks[bank][:, :], ACT.Tanh, scale=0.5), signal=drained[bank])
            yield 2
            pe.wait(f["k_sq"])
            for n in range(GT // 2):
                bank = 2 + n
                product_rows(bank, n, lambda i, t: aT[:, i, t], lambda i: w_v[:, i, :], KD)
                dve.wait(filled[bank], drained[0], drained[1])
                dve.do(lambda e, at, n=n, bank=bank: e.scalar_tensor_tensor(
                    out=tiles(z, n), in0=tiles(z, n), scalar=1.0, in1=banks[bank][:, :],
                    op0=ALU.add, op1=ALU.mult), signal=drained[bank])
            for n in range(GT // 2):
                dve.wait(drained[2 + n])
                dve.do(lambda e, at, n=n: e.scalar_tensor_tensor(
                    out=tiles(x1[:, g, :, :], n), in0=tiles(z, n), scalar=0.5,
                    in1=tiles(x1[:, g, :, :], n), op0=ALU.mult, op1=ALU.add), signal=f["x2_ready"])
            yield 3
            yield from normalize(x1[:, g, :, :], z, f["x2_ready"], [f["diff_ready"], f["mix_ready"]])
            yield 3
            transposed(z, (0, 1), lambda c, bank: lambda e, at: e.activation(
                nT[:, c, 1:1 + G], bank[:, :], ACT.Copy))
            yield 3

        def middle(g):
            dve.wait(f["hc_used"], f["tail_ready"], f["hc_ready"])
            if g == 0:
                dve.do(lambda e, at: e.memset(xpT[:, :, 0:TAPS - 1], 0.0), signal=f["xp_ready"])
            else:
                dve.do(lambda e, at: e.tensor_copy(xpT[:, :, 0:TAPS - 1], xp_tail[:, :, :]),
                       signal=f["xp_ready"])
            pe.wait(drained[0], drained[1])
            for m in range(KE):
                bank = (2, 3, 0, 1)[m]
                product_T(bank, lambda i, m=m: w_in[:, i, m * P:(m + 1) * P],
                          lambda i: nT[:, i, 1:1 + G], KD)
                dve.wait(filled[bank])
                dve.do(lambda e, at, m=m, bank=bank: e.tensor_copy(
                    xpT[:, m, TAPS - 1:TAPS - 1 + G], banks[bank][:, :]), signal=drained[bank])
                yield 1.7
            for m in range(KE):
                bank = (6, 7, 2, 3)[m]
                product_T(bank, lambda i, m=m: w_in[:, i, ED + m * P:ED + (m + 1) * P],
                          lambda i: nT[:, i, 1:1 + G], KD)
                act.wait(filled[bank], f["yg_ready"])
                act.do(lambda e, at, m=m, bank=bank: e.activation(
                    zs[:, m, :], banks[bank][:, :], ACT.Silu), signal=drained[bank])
                yield 1.7
            for m in range(KE):
                bank = (0, 1, 6, 7)[m]
                pe.wait(f["xp_ready"], drained[(2, 3, 0, 1)[m]])
                product_T(bank, lambda i, m=m: conv_diag[:, m, i, :],
                          lambda i, m=m: xpT[:, m, i:i + G], TAPS)
                act.wait(filled[bank])
                act.do(lambda e, at, m=m, bank=bank: e.activation(
                    xc[:, m, :], banks[bank][:, :], ACT.Silu), signal=drained[bank])
                yield 3.4
            if g == 0:
                pool.wait(*drained[0:4])
                pool.do(lambda e, at: e.tensor_copy(xp_tail[:, :, :], xpT[:, :, G:G + TAPS - 1]),
                        apart=True, signal=f["tail_ready"])
            pe.wait(drained[0], drained[1], drained[6], drained[7])
            product_T(LOW, lambda i: w_x[:, i, :], lambda i: xc[:, i, :], KE, rows=RANK + 2 * NS)
            act.wait(filled[LOW], c_stored)
            act.do(lambda e, at: e.activation(dbc[:, :], banks[LOW][0:RANK + 2 * NS, :], ACT.Copy),
                   signal=drained[LOW])
            yield 4
            sp.wait(drained[LOW], *c_landed)
            sp.do(lambda e, at: e.dma_start(c_dram, dbc[RANK + NS:RANK + 2 * NS, :]), signal=c_stored)
            sp.wait(c_stored)
            load_c(0)
            pe.wait(drained[LOW])
            for m in range(KE):
                bank = DT[m]
                product_T(bank, lambda i, m=m: w_dt[:, m * P:(m + 1) * P], lambda i: dbc[0:RANK, :], 1)
                dve.wait(filled[bank])
                dve.do(lambda e, at, m=m, bank=bank: e.tensor_scalar(
                    delta[:, m, :], banks[bank][:, :], col["dt_b"][:, m:m + 1], 40.0, ALU.add, ALU.min),
                    signal=f["sp_in"])
                yield 1
            act.wait(f["sp_in"])
            act.do(lambda e, at: e.activation(delta[:, :, :], delta[:, :, :], ACT.Exp), signal=f["sp_exp"])
            act.wait(f["sp_exp"])
            for m in range(KE):
                act.do(lambda e, at, m=m: e.activation(delta[:, m, :], delta[:, m, :], ACT.Ln, bias=1.0),
                       signal=f["sp_ln"])
            yield 4
            for m in range(KE):
                bank = DT[m]
                dve.wait(but(KE - 1 - m, f["sp_ln"]))
                dve.do(lambda e, at, m=m, bank=bank: e.scalar_tensor_tensor(
                    out=delta[:, m, :], in0=banks[bank][:, :], scalar=col["dt_b"][:, m:m + 1],
                    in1=delta[:, m, :], op0=ALU.add, op1=ALU.max), signal=drained[bank])
            for m in range(KE):
                dve.wait(drained[DT[m]])
                dve.do(lambda e, at, m=m: e.tensor_tensor(
                    u[:, m, :], delta[:, m, :], xc[:, m, :], ALU.mult), signal=f["u_ready"])
            yield 4

        def load_c(block):
            half, n0 = divmod(block, NS // CB)
            sp.wait(f["h_used"])
            sp.do(lambda e, at: e.dma_start(
                c_rows[:, block % 2, :, :],
                c_dram[n0 * CB:(n0 + 1) * CB, half * H:(half + 1) * H].rearrange(
                    "(o n) t -> o n t", o=1).broadcast_to([P, CB, H])), signal=c_landed[block % 2])

        def scan(g):
            steps = [(half, n, part) for half in range(2) for n in range(NS) for part in range(2)]

            def place(k):
                half, n, part = steps[k]
                return half, n, part, slice(2 * part, 2 * part + 2), slice(half * H, (half + 1) * H)

            def rows_b(i):
                half, n, _, _, ts = place(2 * i)
                bank = ROWS_B[i % 2]
                sel = ident[0:RANK + 2 * NS, RANK + n:RANK + n + 1].broadcast_to([RANK + 2 * NS, P])
                pe.wait(drained[bank])
                pe.do(lambda e, at: e.matmul(banks[bank][:, 0:H], sel, dbc[:, ts],
                                             start=True, stop=True), signal=filled[bank])

            def states_behind(k):
                return 0 if k < 3 or (g == GROUPS - 1 and k >= NS * 2) else 2

            def times_b(k):
                half, n, part, es, ts = place(k)
                bank = ROWS_B[k // 2 % 2]
                dve.wait(filled[bank], f["u_ready"], but(2 if k > 1 else 0, f["h_used"]),
                         but(states_behind(k), f["state_ready"]), f["tail_ready"])
                if n % 2:
                    dve.wait(f["hc_ready"])
                dve.do(lambda e, at: e.tensor_tensor(
                    bx[:, k // 2 % 2, es, :], u[:, es, ts],
                    banks[bank][:, 0:H].rearrange("p (o t) -> p o t", o=1).broadcast_to([P, 2, H]),
                    ALU.mult), signal=drained[bank] if part else f["bx_ready"])

            def decays(k):
                half, n, part, es, ts = place(k)
                act.wait(f["u_ready"], but(1 if k > 3 else 0, f["h_ready"]))
                for j in range(2):
                    act.do(lambda e, at, j=j: e.activation(
                        decay[:, k % RING, j, :], delta[:, 2 * part + j, ts], ACT.Exp,
                        scale=a_neg[:, 2 * part + j, n:n + 1]), signal=f["decay_ready"] if j else None)

            def run_h(k):
                half, n, part, es, ts = place(k)
                first = g == 0 and half == 0
                dve.wait(but(min(2, len(steps) - 1 - k), f["decay_ready"]), but(states_behind(k), f["state_ready"]))
                if part == 0 or k == len(steps) - 1:
                    dve.wait(f["bx_ready"], drained[ROWS_B[0]], drained[ROWS_B[1]])
                for j in range(2):
                    m = 2 * part + j
                    dve.do(lambda e, at, j=j, m=m: e.tensor_tensor_scan(
                        bx[:, k // 2 % 2, m, :], decay[:, k % RING, j, :], bx[:, k // 2 % 2, m, :],
                        0.0 if first else state[:, n, m:m + 1], ALU.mult, ALU.add),
                        signal=f["h_ready"] if j else None)

            def times_c(k):
                half, n, part, es, ts = place(k)
                i = k // 2
                pool.wait(f["h_ready"], f["hc_ready"], c_landed[i // CB % 2])
                pool.wait(f["state_ready"] if n % 2 else f["hc_used"])
                pool.do(lambda e, at: e.tensor_tensor(
                    bx[:, 1, es, :] if n % 2 else hc[:, n // 2 % 2, es, :], bx[:, i % 2, es, :],
                    c_rows[:, (i // CB) % 2, i % CB:i % CB + 1, :].broadcast_to([P, 2, H]), ALU.mult),
                    signal=f["h_used"])
                if n % 2 and part:
                    pool.wait(f["h_used"])
                    for p2 in range(2):
                        es2 = slice(2 * p2, 2 * p2 + 2)
                        pool.do(lambda e, at, es2=es2: e.tensor_tensor(
                            hc[:, n // 2 % 2, es2, :], hc[:, n // 2 % 2, es2, :], bx[:, 1, es2, :], ALU.add),
                            signal=f["hc_ready"])

            def keep_state(k):
                half, n, part, es, ts = place(k)
                if not (g == GROUPS - 1 and half == 1):
                    act.wait(f["h_ready"])
                    act.do(lambda e, at: e.activation(
                        state[:, n, es], bx[:, k // 2 % 2, es, H - 1], ACT.Copy), signal=f["state_ready"])

            def sum_n(n):
                pe.wait(f["hc_ready"])
                for part in range(2):
                    bank = Y[part]
                    if n == 1:
                        pe.wait(drained[bank])
                    pe.do(lambda e, at, part=part, bank=bank: e.matmul(
                        banks[bank][:, :], ident[:, :], flat(hc[:, n // 2 % 2, 2 * part:2 * part + 2, :]),
                        start=(n == 1), stop=(n == NS - 1)), signal=f["hc_used"])

            def gate(half):
                ts = slice(half * H, (half + 1) * H)
                for m in range(KE):
                    bank, j = Y[m // 2], m % 2
                    dve.wait(f["hc_used"])
                    dve.do(lambda e, at, m=m, bank=bank, j=j: e.scalar_tensor_tensor(
                        out=xc[:, m, ts], in0=xc[:, m, ts], scalar=col["D"][:, m:m + 1],
                        in1=banks[bank][:, j * H:(j + 1) * H], op0=ALU.mult, op1=ALU.add),
                        signal=drained[bank] if j else None)
                dve.wait(drained[Y[0]], drained[Y[1]], f["decay_ready"])
                dve.do(lambda e, at: e.tensor_tensor(
                    delta[:, :, ts], xc[:, :, ts], zs[:, :, ts], ALU.mult), signal=f["yg_ready"])

            pe.wait(drained[LOW])
            for i in range(2):
                rows_b(i)
            for k in range(2):
                decays(k)
            times_b(0)
            for k in range(len(steps) + 1 + SUM_AT):
                if k < len(steps):
                    if k + 2 < len(steps):
                        decays(k + 2)
                if 0 < k <= len(steps):
                    keep_state(k - 1)
                    times_c(k - 1)
                if k % (2 * CB) == 0 and k // (2 * CB) + 1 < 2 * NS // CB:
                    load_c(k // (2 * CB) + 1)
                if k < len(steps):
                    if k + 1 < len(steps):
                        times_b(k + 1)
                    run_h(k)
                    if k % 2 == 0 and k and k // 2 + 1 < 2 * NS:
                        rows_b(k // 2 + 1)
                if k >= 4 and k % 4 == SUM_AT:
                    sum_n((k - SUM_AT) // 2 % NS - 1 if (k - SUM_AT) // 2 % NS else NS - 1)
                if k > 4 and k % (2 * NS) == SUM_AT:
                    gate((k - SUM_AT) // (2 * NS) - 1)
                yield 1.5

        def back(g):
            pe.wait(f["yg_ready"])
            for n in range(GT // 2):
                bank = TAIL[n]
                product_rows(bank, n, lambda i, t: delta[:, i, t], lambda i: w_out[:, i, :], KE)
                dve.wait(filled[bank], out_stored)
                dve.do(lambda e, at, n=n, bank=bank: e.tensor_tensor(
                    tiles(x3[:, g, :, :], n), banks[bank][:, :], tiles(x1[:, g, :, :], n), ALU.add),
                    signal=drained[bank])
                yield 3.5
            yield from normalize(x3[:, g, :, :], z, drained[TAIL[1]], (), range(6))
            yield 3
            act.wait(f["mean_sum"])
            transposed(z, TAIL, lambda c, bank: lambda e, at: e.activation(
                y4T[:, c, g * G:(g + 1) * G], bank[:, :], ACT.Copy, accum_out=sums[:, g, c:c + 1]))
            yield 3

        def route():
            dve.wait(drained[4], drained[5])
            dve.do(lambda e, at: e.tensor_tensor(mean[:, :], sums[:, 0, :], sums[:, 1, :], ALU.add),
                   signal=f["mean_sum"])
            dve.wait(f["mean_sum"])
            dve.do(lambda e, at: e.tensor_scalar(mean[:, :], mean[:, :], 1.0 / SEQ, None, ALU.mult),
                   signal=f["mean_ready"])
            pe.wait(f["mean_ready"], drained[4])
            for k in range(KD):
                pe.do(lambda e, at, k=k: e.matmul(banks[4][0:1, 0:EXPERTS], mean[:, k:k + 1],
                                                  w_route[:, k, :], start=(k == 0), stop=False))
            pe.do(lambda e, at: e.matmul(banks[4][0:1, 0:EXPERTS], ones_row[:, 0:1], b_route[:, :],
                                         start=False, stop=True), signal=filled[4])
            dve.wait(filled[4], f["pick_ready"])
            dve.do(lambda e, at: e.tensor_copy(scores[:, :], banks[4][0:1, 0:EXPERTS]), signal=drained[4])
            dve.wait(drained[4])
            dve.do(lambda e, at: e.max(top[:, :], scores[:, :]), apart=True, signal=f["max_ready"])
            dve.wait(f["max_ready"])
            dve.do(lambda e, at: e.max_index(top_i[:, :], top[:, :], scores[:, :]), apart=True,
                   signal=f["pick_ready"])
            sp.wait(f["pick_ready"])

            def load_expert(e, at):
                at["pick"] = e.value_load(top_i[0:1, 0:1], min_val=0, max_val=EXPERTS - 1)
                return e.dma_start(w_1[:, :, :], d["W1"][bass.ds(at["pick"], 1)].rearrange(
                    "e (k p) f -> p (e k) f", p=P))

            sp.do(load_expert, signal=w_picked)
            sp.do(lambda e, at: e.dma_start(w_2[:, :, :], d["W2"][bass.ds(at["pick"], 1)].rearrange(
                "e (k p) f -> p (e k) f", p=P)), signal=w_picked)
            sp.do(lambda e, at: e.dma_start(e_b1[:, :], d["b1"][bass.ds(at["pick"], 1)].rearrange(
                "e p k -> (e p) k")), signal=w_picked)
            sp.do(lambda e, at: e.dma_start(e_b2[:, :], d["b2"][bass.ds(at["pick"], 1)]),
                  signal=w_picked)
            yield 10

        def expert(more):
            pe.wait(w_picked, *drained[4:6])
            for g in range(GROUPS):
                for m in range(KM):
                    bank = TAIL[m % 2]
                    product_T(bank, lambda i, m=m: w_1[:, i, m * P:(m + 1) * P],
                              lambda i, g=g: y4T[:, i, g * G:(g + 1) * G], KD)
                    act.wait(filled[bank], w_picked)
                    act.do(lambda e, at, m=m, bank=bank: e.activation(
                        hT[:, m, :], banks[bank][:, :], ACT.Relu, bias=e_b1[:, m:m + 1]),
                        signal=drained[bank])
                    yield 1.7
                pe.wait(*drained[4:6])
                for n in range(GT // 2):
                    bank = TAIL[n]
                    product_rows(bank, n, lambda i, t: hT[:, i, t], lambda i: w_2[:, i, :], KM,
                                 bias=e_b2[:, :])
                    dve.wait(filled[bank], f["ln_out"])
                    dve.do(lambda e, at, g=g, n=n, bank=bank: e.tensor_tensor(
                        tiles(x3[:, g, :, :], n), banks[bank][:, :], tiles(x3[:, g, :, :], n), ALU.add),
                        signal=drained[bank])
                    yield 7
                sp.wait(*drained[4:6])
                sp.do(lambda e, at, g=g: e.dma_start(
                    out_view[bass.ds(at["round"] * GROUPS + g, 1)].rearrange("o p t c -> (o p) t c"),
                    x3[:, g, :, :]), signal=out_stored)
            if more:
                for dst, src in MLP_WEIGHTS:
                    sp.do(lambda e, at, dst=dst, src=src: e.dma_start(dst, src), signal=w_back)

        MLP_WEIGHTS = (
            (w_1[:, :, :], d["mlp_w1T"].rearrange("(k p) n -> p k n", p=P)),
            (w_2[:, :, :], d["mlp_w2T"].rearrange("(k p) n -> p k n", p=P)),
        )

        def alone(stream):
            for _ in stream:
                pass

        def tail(more):
            yield from back(1)
            yield from route()
            if more:
                yield from head()
            yield from expert(more)

        pg.part = "prologue"
        sp.do(lambda e, at: e.dma_start(x_in[:, :, :], x_view[0]), signal=x_landed)
        alone(head())
        alone(front(0, 0, 1))
        alone(middle(0))
        alone(head())
        for part, last in (("body", False), ("epilogue", True)):
            pg.part = part
            interleave(front(0, 1, None if last else GROUPS), scan(0), FRONT_COST, SCAN_COST)
            def back_head():
                yield from back(0)
                if not last:
                    yield from head()
            interleave(middle(1), back_head(), MIDDLE_COST, BACK_COST)
            if last:
                alone(scan(1))
                alone(tail(False))
            else:
                interleave(front(1, 0, GROUPS + 1), scan(1), FRONT_COST, SCAN_COST)
                interleave(middle(0), tail(True), MIDDLE_COST, TAIL_COST)

        block = ctx.enter_context(nc.Block())
        WEIGHTS = (
            (w_qkv[:, :, :], d["w_qkvT"].rearrange("(k p) n -> p k n", p=P)),
            (w_o[:, :, :], d["w_oT"].rearrange("(k p) n -> p k n", p=P)),
            (w_r[:, :, :], d["W_rT"].rearrange("(k p) n -> p k n", p=P)),
            (w_k[:, :, :], d["W_kT"].rearrange("(k p) n -> p k n", p=P)),
            (w_v[:, :, :], d["W_vT"].rearrange("(k p) n -> p k n", p=P)),
            (w_in[:, :, :], d["in_wT"].rearrange("(k p) n -> p k n", p=P)),
            (w_x[:, :, :], d["x_wT"].rearrange("(k p) n -> p k n", p=P)),
            (w_dt[:, :], d["dt_wT"]),
            (w_out[:, :, :], d["out_wT"].rearrange("(k p) n -> p k n", p=P)),
            (w_route[:, :, :], d["Wr"].rearrange("(k p) n -> p k n", p=P)),
            (b_route[:, :], d["br"]),
            (conv_w[:, :, :], d["conv_w"].rearrange("(k p) n -> p k n", p=P)),
            (a_neg[:, :, :], d["A_log"].rearrange("(k p) n -> p k n", p=P)),
            (b2_rows[:, :], d["mlp_b2"].broadcast_to([P, D])),
        ) + MLP_WEIGHTS + tuple((col[n], d[n]) for n in ("ln1_g", "ln1_b", "ln2_g", "ln2_b", "mlp_b1", "mu_r", "mu_k",
                                          "dt_b", "D"))

        def run(e, queue):
            queue.emit(e, "prologue", {"round": 0})
            with e.Fori(0, BATCH - 1) as i:
                queue.emit(e, "body", {"round": i})
            queue.emit(e, "epilogue", {"round": BATCH - 1, "rounds": BATCH - 1})

        def constants(e):
            e.wait_ge(s_w, 16 * len(WEIGHTS))
            e.wait_ge(s_pool, 1)
            e.wait_ge(s_dve, 3)
            e.wait_ge(s_diag, 1)
            e.wait_ge(s_act, 2)

        @block.sync
        def _(e):
            for fl in flags:
                e.sem_inc(fl.sem, CREDIT * fl.step)
            for dst, src in WEIGHTS:
                e.dma_start(dst, src).then_inc(s_w, 16)
            constants(e)
            run(e, sp)
            e.wait_ge(out_stored.sem, out_stored.step * (CREDIT + BATCH * GROUPS))

        @block.gpsimd
        def _(e):
            e.memset(ident[:, :], 0.0).then_inc(s_chain, 1)
            e.memset(band[:, :, :, :], 0.0).then_inc(s_chain, 1)
            e.memset(v_pad[:, :, :, :, :, :], 0.0)
            e.memset(ones_row[:, :], 1.0)
            e.memset(power[:, :], -0.5)
            e.memset(kT[:, :, :], 0.0).then_inc(s_chain, 1)
            e.wait_ge(s_chain, 3)
            e.affine_select(out=ident[:, :], in_=ident[:, :], compare_op=ALU.not_equal, fill=1.0, base=0,
                            pattern=[[-1, P]], channel_multiplier=1).then_inc(s_chain, 1)
            e.affine_select(out=band[:, :, 0, :], in_=band[:, :, 0, :], compare_op=ALU.is_gt, fill=MASKED,
                            base=0, pattern=[[0, 2], [1, P]], channel_multiplier=-1).then_inc(s_chain, 1)
            e.affine_select(out=band[:, :, 1, :], in_=band[:, :, 1, :], compare_op=ALU.is_ge, fill=MASKED,
                            base=0, pattern=[[0, 2], [-1, P]], channel_multiplier=1).then_inc(s_chain, 1)
            e.wait_ge(s_chain, 6)
            e.tensor_copy(ident_bf[:, :], ident[:, :])
            e.tensor_copy(band_first[:, :, :, :], band[:, :, :, :]).then_inc(s_chain, 1)
            e.wait_ge(s_chain, 7)
            e.memset(band_first[:, :, 0, :], MASKED).then_inc(s_pool, 1)
            constants(e)
            run(e, pool)

        @block.vector
        def _(e):
            e.memset(col["own"], 0.0).then_inc(s_dve, 1)
            e.memset(scores[:, :], 0.0)
            e.wait_ge(s_dve, 1)
            for q in range(4):
                e.memset(col["own"][32 * q:32 * q + 16, 2 * q:2 * q + 1], 1.0)
                ins = e.memset(col["own"][32 * q:32 * q + 32, 2 * q + 1:2 * q + 2], 1.0)
            ins.then_inc(s_dve, 1)
            e.wait_ge(s_dve, 2)
            for q in range(4):
                ins = e.memset(col["own"][32 * q:32 * q + 16, 2 * q + 1:2 * q + 2], 0.0)
            ins.then_inc(s_dve, 1)
            e.wait_ge(s_w, 16 * len(WEIGHTS))
            e.wait_ge(s_pool, 1)
            for m in range(KE):
                for k in range(TAPS):
                    ins = e.tensor_scalar(conv_diag[:, m, k, :], ident[:, :], conv_w[:, m, k:k + 1], None,
                                          ALU.mult)
            ins.then_inc(s_diag, 1)
            constants(e)
            run(e, dve)

        @block.scalar
        def _(e):
            e.wait_ge(s_w, 16 * len(WEIGHTS))
            e.activation(a_neg[:, :, :], a_neg[:, :, :], ACT.Exp).then_inc(s_act, 1)
            e.wait_ge(s_act, 1)
            e.activation(a_neg[:, :, :], a_neg[:, :, :], ACT.Copy, scale=-1.0).then_inc(s_act, 1)
            constants(e)
            run(e, act)

        @block.tensor
        def _(e):
            constants(e)
            run(e, pe)


def kernel(**inputs):
    import numpy as np
    import concourse.bacc as bacc
    from concourse.bass_utils import run_bass_kernel_spmd

    a = {n: np.asarray(v) for n, v in inputs.items()}

    def columns(v):
        return np.ascontiguousarray(v.reshape(-1, P).T)

    def transposed(v):
        return np.ascontiguousarray(v.T)

    arrays = {
        "x": a["L0_attn_x"],
        "w_qkvT": transposed(a["L0_attn_w_qkv"]), "w_oT": transposed(a["L0_attn_w_o"]),
        "ln1_g": columns(a["L0_attn_ln1_g"]), "ln1_b": columns(a["L0_attn_ln1_b"]),
        "ln2_g": columns(a["L0_attn_ln2_g"]), "ln2_b": columns(a["L0_attn_ln2_b"]),
        "mlp_w1T": transposed(a["L0_attn_mlp_w1"]), "mlp_b1": columns(a["L0_attn_mlp_b1"]),
        "mlp_w2T": transposed(a["L0_attn_mlp_w2"]), "mlp_b2": a["L0_attn_mlp_b2"].reshape(1, -1),
        "W_rT": transposed(a["L0_ffn_W_r"]), "W_kT": transposed(a["L0_ffn_W_k"]),
        "W_vT": transposed(a["L0_ffn_W_v"]),
        "mu_r": columns(a["L0_ffn_mu_r"]), "mu_k": columns(a["L0_ffn_mu_k"]),
        "in_wT": transposed(a["L1_attn_in_proj_w"]),
        "conv_w": a["L1_attn_conv_w"].reshape(a["L1_attn_conv_w"].shape[0], -1),
        "x_wT": transposed(a["L1_attn_x_proj_w"]), "dt_wT": transposed(a["L1_attn_dt_proj_w"]),
        "dt_b": columns(a["L1_attn_dt_proj_b"]), "A_log": a["L1_attn_A_log"],
        "D": columns(a["L1_attn_D"]), "out_wT": transposed(a["L1_attn_out_proj_w"]),
        "Wr": a["L1_ffn_Wr"], "br": a["L1_ffn_br"].reshape(1, -1),
        "W1": a["L1_ffn_W1"],
        "b1": np.ascontiguousarray(a["L1_ffn_b1"].reshape(a["L1_ffn_b1"].shape[0], -1, P).transpose(0, 2, 1)),
        "W2": a["L1_ffn_W2"], "b2": a["L1_ffn_b2"],
    }
    nc = bacc.Bacc("TRN2", target_bir_lowering=False, num_devices=1)
    d = {n: nc.dram_tensor(f"in_{n}", v.shape, mybir.dt.from_np(v.dtype), kind="ExternalInput").ap()
         for n, v in arrays.items()}
    x = arrays["x"]
    d["out"] = nc.dram_tensor("out_y", x.shape, mybir.dt.from_np(x.dtype), kind="ExternalOutput").ap()
    build_block_stack(nc, d)
    r = run_bass_kernel_spmd(nc, [{f"in_{n}": v for n, v in arrays.items()}], core_ids=[0])
    return r.results[0]["out_y"]
```
